# Optimizing a Trainium2 kernel written in Bass

```python
import numpy as np
import jax
import jax.numpy as jnp

def _softmax(x, axis=-1):
    return jax.nn.softmax(x, axis=axis)

def _gelu(x):
    return jax.nn.gelu(x, approximate=True)

def _silu(x):
    return jax.nn.silu(x)

def _sigmoid(x):
    return jax.nn.sigmoid(x)

def _layernorm(x, axis=-1, eps=1e-05):
    m = jnp.mean(x, axis=axis, keepdims=True)
    v = jnp.var(x, axis=axis, keepdims=True)
    return (x - m) / jnp.sqrt(v + eps)

def _scatter_add(tgt, idx, src, axis=0):
    return tgt.at[idx].add(src)

def _segment_sum(src, seg, n):
    return jax.ops.segment_sum(src, seg, n)
kernel_name = 'mk_macaron_d2_jaxref_r8_224ec2'

def setup_inputs(seed: int=0):
    np.random.seed(seed)
    _w = jnp.asarray

    def _L0_attn_setup():
        import jax, jax.numpy as jnp
        import numpy as np
        D_MODEL = 128
        STATE_DIM = 16
        BATCH = 32
        SEQ = 256

        def _selective_scan(delta, A, B, C):

            def step(state, inp):
                delta_t, B_t, C_t = inp
                state = jnp.exp(A * delta_t) * state + B_t
                y = jnp.sum(state * C_t, axis=-1)
                return (state, y)
            b = delta.shape[0]
            init = jnp.zeros((b, A.shape[0]), dtype=delta.dtype)
            xs = (jnp.swapaxes(delta, 0, 1), jnp.swapaxes(B, 0, 1), jnp.swapaxes(C, 0, 1))
            _, ys = jax.lax.scan(step, init, xs)
            return jnp.swapaxes(ys, 0, 1)
        key = jax.random.key(seed)
        k_x, k_win, k_bin, k_wout, k_bout = jax.random.split(key, 5)
        proj_dim = 2 * D_MODEL + 3 * STATE_DIM
        x = jax.random.normal(k_x, (BATCH, SEQ, D_MODEL), dtype=jnp.float32)
        W_in = jax.random.normal(k_win, (D_MODEL, proj_dim), dtype=jnp.float32) * 0.02
        b_in = jnp.zeros((proj_dim,), dtype=jnp.float32)
        W_out = jax.random.normal(k_wout, (D_MODEL, D_MODEL), dtype=jnp.float32) * 0.02
        b_out = jnp.zeros((D_MODEL,), dtype=jnp.float32)
        A_log = -jnp.log(jnp.arange(1, STATE_DIM + 1, dtype=jnp.float32))
        return {'x': x, 'W_in': W_in, 'b_in': b_in, 'A_log': A_log, 'W_out': W_out, 'b_out': b_out}
    _L0_attn_in = _L0_attn_setup()

    def _L0_ffn_setup():
        import jax, jax.numpy as jnp
        import numpy as np
        LN_EPS = 1e-05

        def layer_norm(x, g, b):
            mu = jnp.mean(x, axis=-1, keepdims=True)
            var = jnp.mean(jnp.square(x - mu), axis=-1, keepdims=True)
            return (x - mu) * jax.lax.rsqrt(var + LN_EPS) * g + b

        def ternary_quant(w):
            scale = 1.0 / jnp.clip(jnp.mean(jnp.abs(w)), 1e-05)
            wq = jnp.clip(jnp.round(w * scale), -1.0, 1.0) / scale
            return w + jax.lax.stop_gradient(wq - w)
        key = jax.random.key(seed)
        ks = jax.random.split(key, 3)
        dim, hidden = (128, 512)
        B, S = (8, 128)
        x = jax.random.normal(ks[0], (B, S, dim), dtype=jnp.float32)
        w1 = jax.random.normal(ks[1], (hidden, dim), dtype=jnp.float32) * 0.02
        w2 = jax.random.normal(ks[2], (dim, hidden), dtype=jnp.float32) * 0.02
        return {'x': x, 'ln1_g': jnp.ones((dim,), jnp.float32), 'ln1_b': jnp.zeros((dim,), jnp.float32), 'w1': w1, 'b1': jnp.zeros((hidden,), jnp.float32), 'ln2_g': jnp.ones((hidden,), jnp.float32), 'ln2_b': jnp.zeros((hidden,), jnp.float32), 'w2': w2, 'b2': jnp.zeros((dim,), jnp.float32)}
    _L0_ffn_in = _L0_ffn_setup()

    def _L1_attn_setup():
        import jax, jax.numpy as jnp
        import numpy as np
        CHUNK = 32
        key = jax.random.key(seed)
        ks = jax.random.split(key, 8)
        d_model, d_inner, n_state, dt_rank, k = (128, 256, 16, 64, 3)
        B, L = (2, 128)
        s = 0.02
        return {'x': jax.random.normal(ks[0], (B, L, d_model), jnp.float32), 'W_in': jax.random.normal(ks[1], (2 * d_inner, d_model), jnp.float32) * s, 'b_in': jnp.zeros((2 * d_inner,), jnp.float32), 'conv_w': jax.random.normal(ks[2], (d_inner, 1, k), jnp.float32) * s, 'conv_b': jnp.zeros((d_inner,), jnp.float32), 'W_x': jax.random.normal(ks[3], (dt_rank + 2 * n_state, d_inner), jnp.float32) * s, 'W_dt': jax.random.normal(ks[4], (d_inner, dt_rank), jnp.float32) * s, 'b_dt': jnp.zeros((d_inner,), jnp.float32), 'A_log': jax.random.normal(ks[5], (d_inner, n_state), jnp.float32), 'W_out': jax.random.normal(ks[6], (d_model, d_inner), jnp.float32) * s, 'b_out': jnp.zeros((d_model,), jnp.float32)}
    _L1_attn_in = _L1_attn_setup()

    def _L1_ffn_setup():
        import jax, jax.numpy as jnp
        import numpy as np
        B, S, D, H, M, E, K = (8, 256, 128, 256, 64, 8, 2)
        EH = H // 2

        def _layernorm(x, g, b, eps=1e-05):
            mu = jnp.mean(x, axis=-1, keepdims=True)
            var = jnp.var(x, axis=-1, keepdims=True)
            return (x - mu) * jax.lax.rsqrt(var + eps) * g + b
        key = jax.random.key(seed)
        ks = jax.random.split(key, 16)
        sc = lambda *shape: 1.0 / np.sqrt(shape[0])
        return {'inputs_embeds': jax.random.normal(ks[0], (B, S, D), jnp.float32), 'W_enc': jax.random.normal(ks[1], (D, H), jnp.float32) * sc(D), 'b_enc': jnp.zeros((H,), jnp.float32), 'W_s2c': jax.random.normal(ks[2], (H, M), jnp.float32) * sc(H), 'b_s2c': jnp.zeros((M,), jnp.float32), 'Wr': jax.random.normal(ks[3], (M, E), jnp.float32) * sc(M), 'br': jnp.zeros((E,), jnp.float32), 'W1': jax.random.normal(ks[4], (E, M, EH), jnp.float32) * sc(M), 'b1': jnp.zeros((E, EH), jnp.float32), 'W2': jax.random.normal(ks[5], (E, EH, M), jnp.float32) * sc(EH), 'b2': jnp.zeros((E, M), jnp.float32), 'W_c2s': jax.random.normal(ks[6], (M, H), jnp.float32) * sc(M), 'b_c2s': jnp.zeros((H,), jnp.float32), 'W_dec': jax.random.normal(ks[7], (H, D), jnp.float32) * sc(H), 'b_dec': jnp.zeros((D,), jnp.float32), 'ln_g': jnp.ones((D,), jnp.float32), 'ln_b': jnp.zeros((D,), jnp.float32)}
    _L1_ffn_in = _L1_ffn_setup()
    _d = {'L0_attn_x': _L0_attn_in['x'], 'L0_attn_W_in': _L0_attn_in['W_in'], 'L0_attn_b_in': _L0_attn_in['b_in'], 'L0_attn_A_log': _L0_attn_in['A_log'], 'L0_attn_W_out': _L0_attn_in['W_out'], 'L0_attn_b_out': _L0_attn_in['b_out'], 'L0_ffn_ln1_g': _L0_ffn_in['ln1_g'], 'L0_ffn_ln1_b': _L0_ffn_in['ln1_b'], 'L0_ffn_w1': _L0_ffn_in['w1'], 'L0_ffn_b1': _L0_ffn_in['b1'], 'L0_ffn_ln2_g': _L0_ffn_in['ln2_g'], 'L0_ffn_ln2_b': _L0_ffn_in['ln2_b'], 'L0_ffn_w2': _L0_ffn_in['w2'], 'L0_ffn_b2': _L0_ffn_in['b2'], 'L1_attn_W_in': _L1_attn_in['W_in'], 'L1_attn_b_in': _L1_attn_in['b_in'], 'L1_attn_conv_w': _L1_attn_in['conv_w'], 'L1_attn_conv_b': _L1_attn_in['conv_b'], 'L1_attn_W_x': _L1_attn_in['W_x'], 'L1_attn_W_dt': _L1_attn_in['W_dt'], 'L1_attn_b_dt': _L1_attn_in['b_dt'], 'L1_attn_A_log': _L1_attn_in['A_log'], 'L1_attn_W_out': _L1_attn_in['W_out'], 'L1_attn_b_out': _L1_attn_in['b_out'], 'L1_ffn_W_enc': _L1_ffn_in['W_enc'], 'L1_ffn_b_enc': _L1_ffn_in['b_enc'], 'L1_ffn_W_s2c': _L1_ffn_in['W_s2c'], 'L1_ffn_b_s2c': _L1_ffn_in['b_s2c'], 'L1_ffn_Wr': _L1_ffn_in['Wr'], 'L1_ffn_br': _L1_ffn_in['br'], 'L1_ffn_W1': _L1_ffn_in['W1'], 'L1_ffn_b1': _L1_ffn_in['b1'], 'L1_ffn_W2': _L1_ffn_in['W2'], 'L1_ffn_b2': _L1_ffn_in['b2'], 'L1_ffn_W_c2s': _L1_ffn_in['W_c2s'], 'L1_ffn_b_c2s': _L1_ffn_in['b_c2s'], 'L1_ffn_W_dec': _L1_ffn_in['W_dec'], 'L1_ffn_b_dec': _L1_ffn_in['b_dec'], 'L1_ffn_ln_g': _L1_ffn_in['ln_g'], 'L1_ffn_ln_b': _L1_ffn_in['ln_b']}
    _x0 = _d['L0_attn_x']
    _d['L0_attn_x'] = jax.random.normal(jax.random.fold_in(jax.random.key(seed), 1), (8, 512, 128), dtype=_x0.dtype)
    del _x0
    return _d

def reference(L0_attn_x, L0_attn_W_in, L0_attn_b_in, L0_attn_A_log, L0_attn_W_out, L0_attn_b_out, L0_ffn_ln1_g, L0_ffn_ln1_b, L0_ffn_w1, L0_ffn_b1, L0_ffn_ln2_g, L0_ffn_ln2_b, L0_ffn_w2, L0_ffn_b2, L1_attn_W_in, L1_attn_b_in, L1_attn_conv_w, L1_attn_conv_b, L1_attn_W_x, L1_attn_W_dt, L1_attn_b_dt, L1_attn_A_log, L1_attn_W_out, L1_attn_b_out, L1_ffn_W_enc, L1_ffn_b_enc, L1_ffn_W_s2c, L1_ffn_b_s2c, L1_ffn_Wr, L1_ffn_br, L1_ffn_W1, L1_ffn_b1, L1_ffn_W2, L1_ffn_b2, L1_ffn_W_c2s, L1_ffn_b_c2s, L1_ffn_W_dec, L1_ffn_b_dec, L1_ffn_ln_g, L1_ffn_ln_b):

    def _L0_attn_ref(x, W_in, b_in, A_log, W_out, b_out):
        import jax, jax.numpy as jnp
        import numpy as np
        D_MODEL = 128
        STATE_DIM = 16
        BATCH = 32
        SEQ = 256

        def _selective_scan(delta, A, B, C):

            def step(state, inp):
                delta_t, B_t, C_t = inp
                state = jnp.exp(A * delta_t) * state + B_t
                y = jnp.sum(state * C_t, axis=-1)
                return (state, y)
            b = delta.shape[0]
            init = jnp.zeros((b, A.shape[0]), dtype=delta.dtype)
            xs = (jnp.swapaxes(delta, 0, 1), jnp.swapaxes(B, 0, 1), jnp.swapaxes(C, 0, 1))
            _, ys = jax.lax.scan(step, init, xs)
            return jnp.swapaxes(ys, 0, 1)
        xz = jnp.einsum('bsd,dp->bsp', x, W_in) + b_in
        d, n = (D_MODEL, STATE_DIM)
        xm = xz[..., :d]
        z = xz[..., d:2 * d]
        Bm = xz[..., 2 * d:2 * d + n]
        Cm = xz[..., 2 * d + n:2 * d + 2 * n]
        delta = jax.nn.softplus(xz[..., 2 * d + 2 * n:])
        A = -jnp.exp(A_log)
        y = _selective_scan(delta, A, Bm, Cm)
        y = y[..., None] * jax.nn.gelu(z, approximate=False)
        return jnp.einsum('bsd,de->bse', y, W_out) + b_out

    def _L0_ffn_ref(x, ln1_g, ln1_b, w1, b1, ln2_g, ln2_b, w2, b2):
        import jax, jax.numpy as jnp
        import numpy as np
        LN_EPS = 1e-05

        def layer_norm(x, g, b):
            mu = jnp.mean(x, axis=-1, keepdims=True)
            var = jnp.mean(jnp.square(x - mu), axis=-1, keepdims=True)
            return (x - mu) * jax.lax.rsqrt(var + LN_EPS) * g + b

        def ternary_quant(w):
            scale = 1.0 / jnp.clip(jnp.mean(jnp.abs(w)), 1e-05)
            wq = jnp.clip(jnp.round(w * scale), -1.0, 1.0) / scale
            return w + jax.lax.stop_gradient(wq - w)
        h = layer_norm(x, ln1_g, ln1_b)
        h = jnp.einsum('bsd,hd->bsh', h, ternary_quant(w1)) + b1
        h = jax.nn.gelu(h, approximate=False)
        h = layer_norm(h, ln2_g, ln2_b)
        out = jnp.einsum('bsh,dh->bsd', h, ternary_quant(w2)) + b2
        return out

    def _L1_attn_ref(x, W_in, b_in, conv_w, conv_b, W_x, W_dt, b_dt, A_log, W_out, b_out):
        import jax, jax.numpy as jnp
        import numpy as np
        CHUNK = 32
        Bsz, L, _ = x.shape
        d_inner, n_state = A_log.shape
        dt_rank = W_dt.shape[1]
        k = conv_w.shape[-1]
        xr = x @ W_in.T + b_in
        xc, res = jnp.split(xr, 2, axis=-1)
        h = jnp.transpose(xc, (0, 2, 1))
        h = jax.lax.conv_general_dilated(h, conv_w, window_strides=(1,), padding=[(k - 1, 0)], dimension_numbers=('NCH', 'OIH', 'NCH'), feature_group_count=d_inner)
        h = h + conv_b[None, :, None]
        u = jax.nn.silu(jnp.transpose(h, (0, 2, 1)))
        xp = u @ W_x.T
        dlt, Bm, Cm = jnp.split(xp, [dt_rank, dt_rank + n_state], axis=-1)
        delta = jax.nn.softplus(dlt @ W_dt.T + b_dt)
        A = -jnp.exp(A_log)
        dA = jnp.exp(jnp.einsum('bld,dn->bldn', delta, A))
        dBu = jnp.einsum('bld,bln,bld->bldn', delta, Bm, u)
        nc = L // CHUNK
        dA_c = dA.reshape(Bsz, nc, CHUNK, d_inner, n_state).transpose(2, 0, 1, 3, 4)
        dBu_c = dBu.reshape(Bsz, nc, CHUNK, d_inner, n_state).transpose(2, 0, 1, 3, 4)
        C_c = Cm.reshape(Bsz, nc, CHUNK, n_state).transpose(2, 0, 1, 3)

        def step(carry, inp):
            a, bu, c = inp
            carry = a * carry + bu
            y = jnp.einsum('bkdn,bkn->bkd', carry, c)
            return (carry, y)
        init = jnp.zeros((Bsz, nc, d_inner, n_state), x.dtype)
        _, ys = jax.lax.scan(step, init, (dA_c, dBu_c, C_c))
        y = ys.transpose(1, 2, 0, 3).reshape(Bsz, L, d_inner)
        y = y * jax.nn.silu(res)
        return y @ W_out.T + b_out

    def _L1_ffn_ref(inputs_embeds, W_enc, b_enc, W_s2c, b_s2c, Wr, br, W1, b1, W2, b2, W_c2s, b_c2s, W_dec, b_dec, ln_g, ln_b):
        import jax, jax.numpy as jnp
        import numpy as np
        B, S, D, H, M, E, K = (8, 256, 128, 256, 64, 8, 2)
        EH = H // 2

        def _layernorm(x, g, b, eps=1e-05):
            mu = jnp.mean(x, axis=-1, keepdims=True)
            var = jnp.var(x, axis=-1, keepdims=True)
            return (x - mu) * jax.lax.rsqrt(var + eps) * g + b
        b, s, d = inputs_embeds.shape
        spikes_enc = jax.nn.sigmoid(inputs_embeds @ W_enc + b_enc)
        flat = spikes_enc.reshape(b * s, -1)
        cont = flat @ W_s2c + b_s2c
        probs = jax.nn.softmax(cont @ Wr + br, axis=-1)
        topk_w, topk_idx = jax.lax.top_k(probs, K)
        topk_w = topk_w / jnp.sum(topk_w, axis=-1, keepdims=True)
        gate = jnp.sum(jax.nn.one_hot(topk_idx, E, dtype=cont.dtype) * topk_w[..., None], axis=1)
        h = jax.nn.relu(jnp.einsum('tm,emh->eth', cont, W1) + b1[:, None, :])
        y = jnp.einsum('eth,ehm->etm', h, W2) + b2[:, None, :]
        expert_out = jnp.einsum('etm,te->tm', y, gate)
        spikes_moe = jax.nn.sigmoid(expert_out @ W_c2s + b_c2s)
        spikes_moe = spikes_moe.reshape(b, s, -1)
        decoded = spikes_moe @ W_dec + b_dec
        return _layernorm(decoded, ln_g, ln_b)
    x = L0_attn_x
    x = x + 0.5 * _L0_ffn_ref(_layernorm(x, axis=-1), L0_ffn_ln1_g, L0_ffn_ln1_b, L0_ffn_w1, L0_ffn_b1, L0_ffn_ln2_g, L0_ffn_ln2_b, L0_ffn_w2, L0_ffn_b2)
    x = x + _L0_attn_ref(_layernorm(x, axis=-1), L0_attn_W_in, L0_attn_b_in, L0_attn_A_log, L0_attn_W_out, L0_attn_b_out)
    x = x + 0.5 * _L0_ffn_ref(_layernorm(x, axis=-1), L0_ffn_ln1_g, L0_ffn_ln1_b, L0_ffn_w1, L0_ffn_b1, L0_ffn_ln2_g, L0_ffn_ln2_b, L0_ffn_w2, L0_ffn_b2)
    x = x + 0.5 * _L1_ffn_ref(_layernorm(x, axis=-1), L1_ffn_W_enc, L1_ffn_b_enc, L1_ffn_W_s2c, L1_ffn_b_s2c, L1_ffn_Wr, L1_ffn_br, L1_ffn_W1, L1_ffn_b1, L1_ffn_W2, L1_ffn_b2, L1_ffn_W_c2s, L1_ffn_b_c2s, L1_ffn_W_dec, L1_ffn_b_dec, L1_ffn_ln_g, L1_ffn_ln_b)
    x = x + _L1_attn_ref(_layernorm(x, axis=-1), L1_attn_W_in, L1_attn_b_in, L1_attn_conv_w, L1_attn_conv_b, L1_attn_W_x, L1_attn_W_dt, L1_attn_b_dt, L1_attn_A_log, L1_attn_W_out, L1_attn_b_out)
    x = x + 0.5 * _L1_ffn_ref(_layernorm(x, axis=-1), L1_ffn_W_enc, L1_ffn_b_enc, L1_ffn_W_s2c, L1_ffn_b_s2c, L1_ffn_Wr, L1_ffn_br, L1_ffn_W1, L1_ffn_b1, L1_ffn_W2, L1_ffn_b2, L1_ffn_W_c2s, L1_ffn_b_c2s, L1_ffn_W_dec, L1_ffn_b_dec, L1_ffn_ln_g, L1_ffn_ln_b)
    return x

_drawn_inputs = setup_inputs


def setup_inputs(seed=0):
    import zlib

    import numpy as np

    out = dict(_drawn_inputs(seed))
    spreads = {'L0_attn_b_in': (0.0, 0.1),
     'L0_attn_b_out': (0.0, 0.1),
     'L0_ffn_ln1_g': (1.0, 0.2),
     'L0_ffn_ln1_b': (0.0, 0.407),
     'L0_ffn_b1': (0.0, 0.1),
     'L0_ffn_ln2_g': (1.0, 0.2),
     'L0_ffn_ln2_b': (0.0, 0.361),
     'L0_ffn_b2': (0.0, 0.1),
     'L1_attn_b_in': (0.0, 0.8),
     'L1_attn_conv_b': (0.0, 0.8),
     'L1_attn_b_dt': (0.0, 0.8),
     'L1_attn_b_out': (0.0, 0.8),
     'L1_ffn_b_enc': (0.0, 1.722),
     'L1_ffn_b_s2c': (0.0, 0.395),
     'L1_ffn_br': (0.0, 0.292),
     'L1_ffn_b1': (0.0, 0.456),
     'L1_ffn_b2': (0.0, 0.335),
     'L1_ffn_b_c2s': (0.0, 0.1),
     'L1_ffn_b_dec': (0.0, 0.1),
     'L1_ffn_ln_g': (1.0, 0.2),
     'L1_ffn_ln_b': (0.0, 0.1)}
    factors = {'L0_attn_A_log': 3.371,
     'L1_attn_W_in': 8.0,
     'L1_attn_conv_w': 8.0,
     'L1_attn_W_x': 8.0,
     'L1_attn_W_dt': 8.0,
     'L1_attn_A_log': 8.0,
     'L1_attn_W_out': 8.0}
    for name, (base, spread) in spreads.items():
        noise = np.random.default_rng([zlib.crc32(name.encode()), seed]).standard_normal(out[name].shape)
        drawn = base * np.exp(spread * noise) if base else spread * noise
        out[name] = jnp.asarray(drawn.astype(out[name].dtype))
    for name, factor in factors.items():
        out[name] = (out[name] * factor).astype(out[name].dtype)
    return out
```

```python
import numpy as np
import concourse.bass as bass
from concourse import mybir
from contextlib import ExitStack

BATCH, SEQ, D = 8, 512, 128
P = 128
TILES = SEQ // P
HIDDEN = 512
HC = HIDDEN // P
STATES = 16
ENC = 256
EC = ENC // P
MOE = 64
EXPERTS = 8
EH = 128
INNER = 256
IC = INNER // P
RANK = 64
CHUNK = 32
TAPS = 3
EPS = 1e-5

F32 = mybir.dt.float32
BF16 = mybir.dt.bfloat16
ALU = mybir.AluOpType
ACT = mybir.ActivationFunctionType
AX = mybir.AxisListType.X


class Signal:

    def __init__(self, sem, per, start=0):
        self.sem, self.per, self.start = sem, per, start

    def at(self, i, n):
        return i * self.per + n + self.start


class Chain:

    def __init__(self, eng, sem, per, i):
        self.eng, self.sem, self.per, self.i, self.n = eng, sem, per, i, 0

    def add(self, ins):
        ins.then_inc(self.sem, 1)
        self.n += 1

    def wait(self):
        self.eng.wait_ge(self.sem, self.i * self.per + self.n)


def build(nc, A, out):
    ctx = ExitStack()
    with ctx:
        def sb(name, shape, dt=F32):
            return ctx.enter_context(nc.sbuf_tensor(name, shape, dt))

        def pb(name, shape, dt=F32):
            return ctx.enter_context(nc.psum_tensor(name, shape, dt))

        def sem(name):
            return ctx.enter_context(nc.semaphore(name))

        ident = sb("ident", [P, P])
        ones = sb("ones", [P, P])
        mean512 = sb("mean512", [P, P])
        neg_half = sb("neg_half", [P, TILES])
        earlier = sb("earlier", [P, EXPERTS, EXPERTS])
        sel = sb("sel", [96, 2 * STATES, P], BF16)
        columns = sb("vectors", [P, N_COLUMNS])
        ln2g, ln2b, b1, b_enc, b_c2s, mb_in, m_cb, mb_dt = (
            columns[:, at:at + n] for at, n in zip(COLUMNS_AT, COLUMNS.values()))
        w1 = sb("w1", [P, HIDDEN])
        w2 = sb("w2", [P, HC, P + 2])
        qs = sb("qs", [P, 8])
        ln1g = sb("ln1g", [P, 1])
        ln1b = sb("ln1b", [P, 1])
        bias2 = sb("bias2", [P, D])
        aw_z = sb("aw_z", [P, D])
        aw_s = sb("aw_s", [P, 96])
        ab_z = sb("ab_z", [P, 1])
        ab_s = sb("ab_s", [96, 1])
        aA = sb("aA", [96, 1])
        aw_o = sb("aw_o", [P, D])
        ab_o = sb("ab_o", [P, D])
        w_enc = sb("w_enc", [P, ENC])
        w_s2c = sb("w_s2c", [P, EC, MOE])
        b_s2c = sb("b_s2c", [MOE, 1])
        w_r = sb("w_r", [MOE + 1, EXPERTS])
        w_e1 = sb("w_e1", [MOE + 1, EXPERTS, EH])
        w_e2 = sb("w_e2", [P, EXPERTS, MOE])
        b_e2 = sb("b_e2", [MOE, EXPERTS])
        w_c2s = sb("w_c2s", [MOE + EXPERTS, ENC])
        w_dec = sb("w_dec", [P, EC, D])
        b_dec = sb("b_dec", [P, D])
        mlng = sb("mlng", [P, D])
        mlnb = sb("mlnb", [P, D])
        mw_in = sb("mw_in", [P, 2 * INNER])
        m_cw = sb("m_cw", [P, IC, TAPS])
        mw_x = sb("mw_x", [P, IC, RANK + 2 * STATES])
        mw_dt = sb("mw_dt", [RANK, INNER])
        mA = sb("mA", [P, IC, STATES])
        mw_o = sb("mw_o", [P, IC, D])
        mb_o = sb("mb_o", [P, D])

        loads = sem("loads")
        iota_done = sem("iota_done")
        pool_const = sem("pool_const")
        dve_setup = sem("dve_setup")
        act_setup = sem("act_setup")
        pe_setup = sem("pe_setup")

        class Thread:

            def __init__(self, n, lns, moes, ffns, updates, wide):
                self.n = n
                self.he = wide
                self.x = sb(n + "x", [P, TILES, D])
                self.xp = sb(n + "xp", [P, TILES, D])
                self.st = sb(n + "st", [P, TILES, 6])
                self.mv = sb(n + "mv", [P, TILES, 2])
                self.vv = sb(n + "vv", [P, TILES])
                self.rs = sb(n + "rs", [P, TILES])
                self.z = sb(n + "z", [P, TILES, D])
                self.zT = sb(n + "zT", [P, SEQ])
                self.ps = [pb(f"{n}ps{k}", [P, 512]) for k in range(2)]
                self.po = [pb(f"{n}po{k}", [P, 512]) for k in range(2)]
                norms = lns + moes + ffns
                self.var = Signal(sem(n + "var"), norms)
                self.rstd = Signal(sem(n + "rstd"), norms)
                self.xpre = Signal(sem(n + "xpre"), lns)
                self.x_new = Signal(sem(n + "x_new"), updates, 1)
                self.zn = Signal(sem(n + "zn"), lns * TILES)
                self.zt_ps = Signal(sem(n + "zt_ps"), lns)
                self.zt = Signal(sem(n + "zt"), lns)
                self.s1 = sb(n + "s1", [P, EC, SEQ])
                self.cont = sb(n + "cont", [MOE + 1, SEQ])
                self.lg = sb(n + "lg", [P, TILES, EXPERTS])
                self.mx = sb(n + "mx", [P, TILES])
                self.ex = sb(n + "ex", [P, TILES, EXPERTS])
                self.cmp = sb(n + "cmp", [P, TILES, EXPERTS, EXPERTS])
                self.eq = sb(n + "eq", [P, TILES, EXPERTS, EXPERTS])
                self.rk = sb(n + "rk", [P, TILES, EXPERTS])
                self.sm = sb(n + "sm", [P, TILES])
                self.eo = sb(n + "eo", [P, TILES, MOE + EXPERTS])
                self.gy = sb(n + "gy", [P, EXPERTS, MOE])
                self.eoT = sb(n + "eoT", [MOE + EXPERTS, SEQ])
                self.dd = sb(n + "dd", [P, TILES, D])
                self.enc_ps = Signal(sem(n + "enc_ps"), moes * EC)
                self.s1r = Signal(sem(n + "s1r"), moes * EC)
                self.cont_ps = Signal(sem(n + "cont_ps"), moes)
                self.contr = Signal(sem(n + "contr"), moes)
                self.route_ps = Signal(sem(n + "route_ps"), moes)
                self.lgr = Signal(sem(n + "lgr"), moes)
                self.exr = Signal(sem(n + "exr"), moes)
                self.he_ps = Signal(sem(n + "he_ps"), moes * EXPERTS)
                self.her = Signal(sem(n + "her"), moes * EXPERTS)
                self.ye_ps = Signal(sem(n + "ye_ps"), moes * TILES)
                self.yer = Signal(sem(n + "yer"), moes * TILES)
                self.eor = Signal(sem(n + "eor"), moes)
                self.eoT_ps = Signal(sem(n + "eoT_ps"), moes)
                self.eoTr = Signal(sem(n + "eoTr"), moes)
                self.c2s_ps = Signal(sem(n + "c2s_ps"), moes * EC)
                self.s2r = Signal(sem(n + "s2r"), moes * EC)
                self.dec_ps = Signal(sem(n + "dec_ps"), moes)
                self.ddn = Signal(sem(n + "ddn"), moes)
                self.ddg = Signal(sem(n + "ddg"), moes)

        fwide = sb("fwide", [P, EXPERTS, SEQ])
        bwide = sb("bwide", [P, EXPERTS, SEQ])
        FR = Thread("f_", 4, 1, 2, 3, fwide)
        BK = Thread("b_", 2, 1, 0, 2, bwide)
        w1q, tmp, tmp2 = FR.s1[:, 0, :], BK.s1[:, 0, :], BK.s1[:, 1, :]
        w2q = FR.s1[:, 1, :].rearrange("p (c d) -> p c d", c=HC)
        xin = sb("xin", [P, TILES, D])
        hT = fwide[:, 0:HC, :]
        sq = fwide[:, HC:2 * HC, :]
        fs = sb("fs", [P, 2, 2, 2])
        fvar = sb("fvar", [P, TILES])
        frs = sb("frs", [P, TILES])
        gz = sb("gz", [P, SEQ])
        bcd = sb("bcd", [96, SEQ])
        adt = sb("adt", [96, 3, SEQ])
        adA = sb("adA", [STATES, SEQ])
        ah = sb("ah", [64, SEQ])
        ap_ = sb("ap_", [64, SEQ])
        ay = sb("ay", [P, TILES])
        x_in = Signal(sem("x_in"), 16)
        h_ps = Signal(sem("h_ps"), 2 * HC)
        h_r = Signal(sem("h_r"), 2 * HC)
        sq_r = Signal(sem("sq_r"), 2 * HC)
        fo_ps = Signal(sem("fo_ps"), 2)
        az_ps = Signal(sem("az_ps"), 1)
        as_ps = Signal(sem("as_ps"), 1)
        bcd_r = Signal(sem("bcd_r"), 1)
        gz_r = Signal(sem("gz_r"), 1)
        aln_r = Signal(sem("aln_r"), 1)
        adelta_r = Signal(sem("adelta_r"), 1)
        adA_r = Signal(sem("adA_r"), 1)
        ap_r = Signal(sem("ap_r"), 1)
        ao_ps = Signal(sem("ao_ps"), 1)
        xc = sb("xc", [P, IC, SEQ + TAPS - 1])
        res = sb("res", [P, IC, SEQ])
        rth = sb("rth", [P, IC, SEQ])
        cv = sb("cv", [P, 2, IC, SEQ])
        u2 = sb("u2", [P, IC, SEQ])
        g4 = sb("g4", [P, IC, SEQ])
        dlt = sb("dlt", [RANK, SEQ])
        bc = sb("bc", [96, 3, SEQ])
        bch = sb("bch", [96, 2, SEQ], BF16)
        bc3 = sb("bc3", [96, SEQ], BF16)
        dab = sb("dab", [P, IC, SEQ])
        dex = sb("dex", [P, IC, SEQ])
        cth = dex
        delta = sb("delta", [P, IC, SEQ])
        du = cv[:, 1, :, :]
        dA = sb("dA", [P, 2, IC * SEQ])
        bbc = sb("bbc", [P, 2, SEQ])
        dbu = sb("dbu", [P, 2, IC * SEQ])
        hs = bwide[:, 0:4, :].rearrange("p (b c) t -> p b (c t)", b=2)
        hc = bwide[:, 4:8, :].rearrange("p (b c) t -> p b (c t)", b=2)
        yg = u2
        xo = sb("xo", [P, TILES, D])
        handed = Signal(sem("handed"), 1)
        min_ps = Signal(sem("min_ps"), 2 * IC)
        min_r = Signal(sem("min_r"), 2 * IC)
        rth_r = Signal(sem("rth_r"), 1)
        cv_r = Signal(sem("cv_r"), 1)
        cth_r = Signal(sem("cth_r"), 1)
        u2_r = Signal(sem("u2_r"), 1)
        mx_ps = Signal(sem("mx_ps"), 1)
        dlt_r = Signal(sem("dlt_r"), 1)
        bcf_r = Signal(sem("bcf_r"), 1)
        bc3_r = Signal(sem("bc3_r"), 3)
        mdt_ps = Signal(sem("mdt_ps"), IC)
        mrelu_r = Signal(sem("mrelu_r"), IC)
        mabs_r = Signal(sem("mabs_r"), IC)
        mln_r = Signal(sem("mln_r"), 1)
        delta_r = Signal(sem("delta_r"), 1)
        du_r = Signal(sem("du_r"), 1)
        dA_r = Signal(sem("dA_r"), STATES)
        bbc_ps = Signal(sem("bbc_ps"), STATES)
        bbc_r = Signal(sem("bbc_r"), STATES)
        cbc_ps = Signal(sem("cbc_ps"), STATES)
        dbu_r = Signal(sem("dbu_r"), STATES)
        hs_r = Signal(sem("hs_r"), STATES)
        hc_r = Signal(sem("hc_r"), STATES)
        sum_ps = Signal(sem("sum_ps"), STATES)
        yg_r = Signal(sem("yg_r"), 1)
        mo_ps = Signal(sem("mo_ps"), 1)
        xo_free = Signal(sem("xo_free"), 16, 1)
        dve_f, dve_b = sem("dve_f"), sem("dve_b")
        act_f, act_b = sem("act_f"), sem("act_b")

        block = ctx.enter_context(nc.Block())
        row = lambda ap: ap.rearrange("(a n) -> a n", a=1)
        col = lambda ap: ap.rearrange("(p a) -> p a", a=1)
        tiles = lambda ap: ap.rearrange("(q p) d -> p q d", p=P)
        NLOADS = [0]

        @block.sync
        def _(sp):
            def load(dst, src):
                sp.dma_start(dst, src).then_inc(loads, 16)
                NLOADS[0] += 1

            load(w1[:, :], A["w1T"])
            load(tmp2[:, :], A["w2T"])
            load(columns[:, :], A["columns"])
            load(ln1g[:, :], col(A["L0_ffn_ln1_g"]))
            load(ln1b[:, :], col(A["L0_ffn_ln1_b"]))
            load(bias2[:, :], row(A["L0_ffn_b2"]).broadcast_to([P, D]))
            load(aw_z[:, :], A["L0_attn_W_in"][:, D:2 * D])
            load(ab_z[:, :], col(A["L0_attn_b_in"][D:2 * D]))
            load(aw_o[:, :], A["L0_attn_W_out"])
            load(ab_o[:, :], row(A["L0_attn_b_out"]).broadcast_to([P, D]))
            load(w_enc[:, :], A["L1_ffn_W_enc"])
            load(w_s2c[:, :, :], A["L1_ffn_W_s2c"].rearrange("(c p) m -> p c m", p=P))
            load(b_s2c[:, :], col(A["L1_ffn_b_s2c"]))
            load(w_r[0:MOE, :], A["L1_ffn_Wr"])
            load(w_r[MOE:MOE + 1, :], row(A["L1_ffn_br"]))
            load(w_e1[0:MOE, :, :], A["L1_ffn_W1"].rearrange("e m h -> m e h"))
            load(w_e1[MOE:MOE + 1, :, :], A["L1_ffn_b1"].rearrange("(a e) h -> a e h", a=1))
            load(w_e2[:, :, :], A["L1_ffn_W2"].rearrange("e h m -> h e m"))
            load(b_e2[:, :], A["moe_b2T"])
            load(w_c2s[0:MOE, :], A["L1_ffn_W_c2s"])
            load(w_dec[:, :, :], A["L1_ffn_W_dec"].rearrange("(c p) d -> p c d", p=P))
            load(b_dec[:, :], row(A["L1_ffn_b_dec"]).broadcast_to([P, D]))
            load(mlng[:, :], row(A["L1_ffn_ln_g"]).broadcast_to([P, D]))
            load(mlnb[:, :], row(A["L1_ffn_ln_b"]).broadcast_to([P, D]))
            load(mw_in[:, :], A["mamba_W_inT"])
            load(m_cw[:, :, :], A["L1_attn_conv_w"].rearrange("(c p) a k -> p c (a k)", p=P))
            load(mw_x[:, :, :], A["mamba_W_xT"].rearrange("(c p) m -> p c m", p=P))
            load(mw_dt[:, :], A["mamba_W_dtT"])
            load(mA[:, :, :], A["L1_attn_A_log"].rearrange("(c p) n -> p c n", p=P))
            load(mw_o[:, :, :], A["mamba_W_outT"].rearrange("(c p) d -> p c d", p=P))
            load(mb_o[:, :], row(A["L1_attn_b_out"]).broadcast_to([P, D]))
            sp.wait_ge(pool_const, 1)
            for k in range(3):
                at, of = 32 * k, 2 * D + STATES * k
                load(aw_s[:, at:at + STATES], A["L0_attn_W_in"][:, of:of + STATES])
                load(ab_s[at:at + STATES, :], col(A["L0_attn_b_in"][of:of + STATES]))
            load(aA[64:64 + STATES, :], col(A["L0_attn_A_log"]))
            assert NLOADS[0] == N_LOADS

            sp.dma_start(xin[:, :, :], tiles(A["L0_attn_x"][0, :, :])).then_inc(x_in.sem, 16)
            with sp.Fori(1, BATCH) as i:
                sp.wait_ge(FR.x_new.sem, FR.x_new.at(i - 1, 1))
                sp.dma_start(xin[:, :, :], tiles(A["L0_attn_x"][i, :, :])).then_inc(x_in.sem, 16)
                sp.wait_ge(BK.x_new.sem, BK.x_new.at(i, 0))
                sp.dma_start(tiles(out[i - 1, :, :]), xo[:, :, :]).then_inc(xo_free.sem, 16)
            sp.wait_ge(BK.x_new.sem, BK.x_new.at(BATCH, 0))
            sp.dma_start(tiles(out[BATCH - 1, :, :]), xo[:, :, :]).then_inc(xo_free.sem, 16)
            sp.wait_ge(xo_free.sem, xo_free.at(BATCH, 0))

        @block.gpsimd
        def _(pool):
            n = [0]

            def step(ins):
                ins.then_inc(iota_done, 1)
                n[0] += 1
                pool.wait_ge(iota_done, n[0])

            step(pool.memset(ab_s[:, :], 0.0))
            step(pool.memset(aA[:, :], 0.0))
            pool.memset(aw_s[:, :], 0.0).then_inc(pool_const, 1)
            pool.wait_ge(pool_const, 1)
            step(pool.memset(ones[:, :], 1.0))
            step(pool.memset(mean512[:, :], 1.0 / HIDDEN))
            step(pool.memset(neg_half[:, :], -0.5))
            step(pool.memset(xc[:, :, 0:TAPS - 1], 0.0))
            step(pool.memset(FR.cont[MOE:MOE + 1, :], 1.0))
            step(pool.memset(BK.cont[MOE:MOE + 1, :], 1.0))
            for k in range(2):
                starts = dA[:, k, :].rearrange("p (c t) -> p c t", t=CHUNK)[:, :, 0:1]
                step(pool.memset(starts, 0.0))
            step(pool.memset(ident[:, :], 0.0))
            step(pool.affine_select(out=ident[:, :], in_=ident[:, :], compare_op=ALU.not_equal, fill=1.0,
                                    base=0, pattern=[[-1, P]], channel_multiplier=1))
            step(pool.memset(earlier[:, :, :], 0.0))
            step(pool.affine_select(out=earlier[:, :, :], in_=earlier[:, :, :], compare_op=ALU.is_ge, fill=1.0,
                                    base=0, pattern=[[-1, EXPERTS], [1, EXPERTS]], channel_multiplier=0))
            step(pool.memset(sel[:, :, :], 0.0))
            for piece in range(3):
                step(pool.affine_select(out=sel[:, :, :], in_=sel[:, :, :], compare_op=ALU.not_equal, fill=1.0,
                                        base=-32 * piece, pattern=[[-1, 2 * STATES], [0, P]],
                                        channel_multiplier=1))
            pool.memset(w2[:, :, P:P + 2], 1.0 / HIDDEN).then_inc(pool_const, 1)
            pool.wait_ge(dve_setup, 2)

            def rstd(T, i, k, src, dst):
                pool.wait_ge(T.var.sem, T.var.at(i, k + 1))
                pool.tensor_tensor(out=dst, in0=src, in1=neg_half[:, :], op=ALU.pow).then_inc(T.rstd.sem, 1)

            def pre_add(T, i, l, x, bias, after):
                after()
                b = bias[:, :].rearrange("p (a d) -> p a d", a=1).broadcast_to([P, TILES, D])
                pool.tensor_tensor(out=T.xp[:, :, :], in0=x[:, :, :], in1=b,
                                   op=ALU.add).then_inc(T.xpre.sem, 1)

            def front(i):
                T = FR
                pre_add(T, i, 0, xin, bias2, lambda: (pool.wait_ge(x_in.sem, x_in.at(i, 16)),
                                                      pool.wait_ge(T.x_new.sem, T.x_new.at(i, 0))))
                rstd(T, i, 0, T.vv[:, :], T.rs[:, :])
                rstd(T, i, 1, fvar[:, :], frs[:, :])
                pre_add(T, i, 1, T.x, ab_o, lambda: pool.wait_ge(T.x_new.sem, T.x_new.at(i, 1)))
                rstd(T, i, 2, T.vv[:, :], T.rs[:, :])
                pre_add(T, i, 2, T.x, bias2, lambda: pool.wait_ge(T.x_new.sem, T.x_new.at(i, 2)))
                rstd(T, i, 3, T.vv[:, :], T.rs[:, :])
                rstd(T, i, 4, fvar[:, :], frs[:, :])
                pre_add(T, i, 3, T.x, mlnb, lambda: pool.wait_ge(T.x_new.sem, T.x_new.at(i, 3)))
                rstd(T, i, 5, T.vv[:, :], T.rs[:, :])
                moe(T, i, 6)

            def moe(T, i, k):
                rstd(T, i, k, T.vv[:, :], T.rs[:, :])
                pool.wait_ge(T.ddn.sem, T.ddn.at(i, 1))
                g = mlng[:, :].rearrange("p (a d) -> p a d", a=1).broadcast_to([P, TILES, D])
                pool.tensor_tensor(out=T.dd[:, :, :], in0=T.dd[:, :, :], in1=g,
                                   op=ALU.mult).then_inc(T.ddg.sem, 1)

            def back(i):
                T = BK
                pre_add(T, i, 0, T.x, mb_o, lambda: (pool.wait_ge(handed.sem, handed.at(i, 1)),
                                                     pool.wait_ge(T.x_new.sem, T.x_new.at(i, 0))))
                rstd(T, i, 0, T.vv[:, :], T.rs[:, :])
                pool.wait_ge(du_r.sem, du_r.at(i, 1))
                for n_ in range(STATES):
                    b = n_ % 2
                    pool.wait_ge(bbc_r.sem, bbc_r.at(i, n_ + 1))
                    if n_ >= 2:
                        pool.wait_ge(hs_r.sem, hs_r.at(i, n_ - 1))
                    in1 = bbc[:, b, :].rearrange("p (a t) -> p a t", a=1).broadcast_to([P, IC, SEQ])
                    pool.tensor_tensor(out=dbu[:, b, :].rearrange("p (c t) -> p c t", c=IC),
                                       in0=du[:, :, :], in1=in1, op=ALU.mult).then_inc(dbu_r.sem, 1)
                pre_add(T, i, 1, T.x, mlnb, lambda: pool.wait_ge(T.x_new.sem, T.x_new.at(i, 1)))
                rstd(T, i, 1, T.vv[:, :], T.rs[:, :])
                moe(T, i, 2)

            with pool.Fori(0, BATCH) as i:
                front(i)
                back(i)

        @block.vector
        def _(dve):
            n = [0]

            def step(ins):
                ins.then_inc(dve_f, 1)
                n[0] += 1
                dve.wait_ge(dve_f, n[0])

            dve.wait_ge(loads, 16 * N_LOADS)
            dve.wait_ge(pool_const, 2)
            w2v = tmp2[:, :]
            dve.wait_ge(pe_setup, 2)
            for k, w in enumerate((w1[:, :], w2v)):
                q = qs[:, 4 * k:4 * k + 4]
                step(dve.tensor_scalar(out=q[:, 0:1], in0=FR.ps[k][:, 0:1], scalar1=1.0 / (D * HIDDEN),
                                       scalar2=1e-5, op0=ALU.mult, op1=ALU.max))
                step(dve.reciprocal(out=q[:, 1:2], in_=q[:, 0:1]))
                step(dve.tensor_scalar(out=tmp[:, :], in0=w, scalar1=q[:, 1:2], scalar2=-0.5,
                                       op0=ALU.mult, op1=ALU.is_lt))
                step(dve.tensor_scalar(out=w, in0=w, scalar1=q[:, 1:2], scalar2=0.5,
                                       op0=ALU.mult, op1=ALU.is_gt))
                step(dve.tensor_tensor(out=w, in0=w, in1=tmp[:, :], op=ALU.subtract))
                dst = w1q[:, :] if k == 0 else w2q[:, :, :].rearrange("p c d -> p (c d)")
                step(dve.tensor_scalar(out=dst, in0=w, scalar1=q[:, 0:1], scalar2=None, op0=ALU.mult))
            step(dve.tensor_scalar(out=w1[:, :], in0=w1q[:, :], scalar1=ln1g[:, 0:1], scalar2=None, op0=ALU.mult))
            for c in range(HC):
                step(dve.tensor_scalar(out=w2[:, c, 0:P], in0=w2q[:, c, :], scalar1=ln2g[:, c:c + 1],
                                       scalar2=None, op0=ALU.mult))
                step(dve.tensor_scalar(out=tmp[:, c * P:(c + 1) * P], in0=w2q[:, c, :],
                                       scalar1=ln2b[:, c:c + 1], scalar2=None, op0=ALU.mult))
            for a in (b_enc[:, :], w_s2c[:, :, :], b_c2s[:, :], w_dec[:, :, :], mlng[:, :], mlnb[:, :],
                      mw_x[:, :, :]):
                step(dve.tensor_scalar(out=a, in0=a, scalar1=0.5, scalar2=None, op0=ALU.mult))
            step(dve.tensor_scalar(out=mw_o[:, :, :], in0=mw_o[:, :, :], scalar1=0.25, scalar2=None, op0=ALU.mult))
            dve.wait_ge(act_setup, 4)
            step(dve.tensor_scalar(out=mA[:, :, :], in0=mA[:, :, :], scalar1=-1.0, scalar2=None, op0=ALU.mult))
            step(dve.tensor_scalar(out=aA[:, :], in0=aA[:, :], scalar1=-1.0, scalar2=None, op0=ALU.mult))
            dve.memset(qs[:, 3:4], 0.0).then_inc(dve_setup, 1)
            dve.wait_ge(pe_setup, 3)
            for c in range(HC):
                step(dve.tensor_tensor(out=w2[:, c, 0:P], in0=w2[:, c, 0:P], in1=FR.po[0][:, 0:P],
                                       op=ALU.subtract))
            step(dve.tensor_tensor(out=bias2[:, :], in0=bias2[:, :], in1=FR.po[0][:, P:2 * P], op=ALU.add))
            step(dve.tensor_scalar(out=bias2[:, :], in0=bias2[:, :], scalar1=0.5, scalar2=None, op0=ALU.mult))
            step(dve.tensor_tensor(out=b1[:, :], in0=b1[:, :], in1=FR.po[0][:, 2 * P:2 * P + HC], op=ALU.add))
            step(dve.tensor_tensor(out=b_dec[:, :], in0=b_dec[:, :], in1=FR.po[1][:, 0:P], op=ALU.add))
            step(dve.tensor_tensor(out=b_s2c[:, :], in0=b_s2c[:, :], in1=FR.po[1][0:MOE, P:P + 1], op=ALU.add))
            step(dve.tensor_copy(out=w_c2s[MOE:MOE + EXPERTS, :], in_=FR.ps[1][0:EXPERTS, 0:ENC]))
            dve.memset(qs[:, 3:4], 0.0).then_inc(dve_setup, 1)
            SET = n[0]
            for sig in (FR.x_new, BK.x_new, xo_free):
                dve.sem_inc(sig.sem, sig.start)

            def norm(T, ch, i, l, k, x, double, sig=None):
                for q in range(TILES):
                    ch.add(dve.bn_stats(out=T.st[:, q, :], in_=x[:, q, :]))
                ch.wait()
                dve.memset(T.vv[:, 0:1], 0.0)
                for q in range(TILES):
                    ch.add(dve.bn_aggr(out=T.mv[:, q, :], in_=T.st[:, q, :]))
                ch.wait()
                s1, s2 = (1.0 + EPS, EPS * EPS) if double else (1.0, EPS)
                dve.tensor_scalar(out=T.vv[:, :], in0=T.mv[:, :, 1], scalar1=s1, scalar2=s2,
                                  op0=ALU.mult, op1=ALU.add).then_inc(T.var.sem, 1)
                dve.wait_ge(T.rstd.sem, T.rstd.at(i, k + 1))
                for q in range(TILES):
                    ins = dve.tensor_scalar(out=(T.z if sig is None else T.dd)[:, q, :], in0=x[:, q, :],
                                            scalar1=T.mv[:, q, 0:1], scalar2=T.rs[:, q:q + 1],
                                            op0=ALU.subtract, op1=ALU.mult)
                    if sig is None:
                        ins.then_inc(T.zn.sem, 1)
                    elif q < TILES - 1:
                        ch.add(ins)
                    else:
                        ins.then_inc(sig.sem, 1)

            def ffn(ch, i, f, l, k, x, x_ready):
                T = FR
                x_ready()
                norm(T, ch, i, l, k, x, True)
                for c in range(HC):
                    dve.wait_ge(h_r.sem, h_r.at(i, f * HC + c + 1))
                    dve.tensor_tensor(out=sq[:, c, :], in0=hT[:, c, :], in1=hT[:, c, :],
                                      op=ALU.mult).then_inc(sq_r.sem, 1)
                dve.wait_ge(fo_ps.sem, fo_ps.at(i, f + 1))
                for b in range(2):
                    stat = T.po[b][:, :].rearrange("p (q n) -> p q n", q=2)[:, :, P:P + 2]
                    ch.add(dve.tensor_copy(out=fs[:, b, :, :], in_=stat))
                ch.wait()
                mean = fs[:, :, :, 0]
                ch.add(dve.tensor_tensor(out=fvar[:, :].rearrange("p (b q) -> p b q", b=2), in0=mean, in1=mean,
                                         op=ALU.mult))
                ch.wait()
                ch.add(dve.scalar_tensor_tensor(out=fvar[:, :].rearrange("p (b q) -> p b q", b=2),
                                                in0=fs[:, :, :, 1], scalar=EPS,
                                                in1=fvar[:, :].rearrange("p (b q) -> p b q", b=2),
                                                op0=ALU.add, op1=ALU.subtract))
                ch.wait()
                dve.tensor_scalar(out=fvar[:, :], in0=fvar[:, :], scalar1=EPS, scalar2=None,
                                  op0=ALU.max).then_inc(T.var.sem, 1)
                dve.wait_ge(T.rstd.sem, T.rstd.at(i, k + 2))
                ch.add(dve.tensor_scalar(out=frs[:, :], in0=frs[:, :], scalar1=0.5, scalar2=None, op0=ALU.mult))
                ch.wait()
                dve.wait_ge(T.xpre.sem, T.xpre.at(i, l + 1))
                for q in range(TILES):
                    src = T.po[q // 2][:, (q % 2) * 256:(q % 2) * 256 + D]
                    ins = dve.scalar_tensor_tensor(out=T.x[:, q, :], in0=src, scalar=frs[:, q:q + 1],
                                                   in1=T.xp[:, q, :], op0=ALU.mult, op1=ALU.add)
                    if q < TILES - 1:
                        ch.add(ins)
                    else:
                        ins.then_inc(T.x_new.sem, 1)

            def attn(ch, i):
                T = FR
                dve.wait_ge(T.x_new.sem, T.x_new.at(i, 1))
                norm(T, ch, i, 1, 2, T.x, False)
                R = slice(64, 64 + STATES)
                dve.wait_ge(bcd_r.sem, bcd_r.at(i, 1))
                dve.wait_ge(aln_r.sem, aln_r.at(i, 1))
                dve.scalar_tensor_tensor(out=adt[R, 2, :], in0=bcd[R, :], scalar=0.0, in1=adt[R, 1, :],
                                         op0=ALU.max, op1=ALU.add).then_inc(adelta_r.sem, 1)
                dve.wait_ge(adA_r.sem, adA_r.at(i, 1))
                ch.add(dve.tensor_tensor_scan(out=ah[32:32 + STATES, :], data0=adA[:, :], data1=bcd[0:STATES, :],
                                              initial=0.0, op0=ALU.mult, op1=ALU.add))
                ch.wait()
                dve.tensor_tensor(out=ap_[32:32 + STATES, :], in0=ah[32:32 + STATES, :],
                                  in1=bcd[32:32 + STATES, :], op=ALU.mult).then_inc(ap_r.sem, 1)
                dve.wait_ge(ao_ps.sem, ao_ps.at(i, 1))
                ch.add(dve.tensor_copy(out=ay[:, :], in_=T.po[1][:, 0:TILES]))
                ch.wait()
                dve.wait_ge(T.xpre.sem, T.xpre.at(i, 2))
                for q in range(TILES):
                    ins = dve.scalar_tensor_tensor(out=T.x[:, q, :], in0=T.po[0][:, q * D:(q + 1) * D],
                                                   scalar=ay[:, q:q + 1], in1=T.xp[:, q, :],
                                                   op0=ALU.mult, op1=ALU.add)
                    if q < TILES - 1:
                        ch.add(ins)
                    else:
                        ins.then_inc(T.x_new.sem, 1)

            def moe(T, ch, i, l, k, dst, dst_sem, free):
                dve.wait_ge(T.x_new.sem, T.x_new.at(i, l))
                norm(T, ch, i, l, k, T.x, False)
                dve.wait_ge(T.cont_ps.sem, T.cont_ps.at(i, 1))
                dve.tensor_scalar(out=T.cont[0:MOE, :], in0=T.ps[0][0:MOE, :], scalar1=b_s2c[:, :],
                                  scalar2=None, op0=ALU.add).then_inc(T.contr.sem, 1)
                dve.wait_ge(T.route_ps.sem, T.route_ps.at(i, 1))
                lgr = T.po[0][:, 0:TILES * EXPERTS].rearrange("p (q e) -> p q e", q=TILES)
                ch.add(dve.tensor_copy(out=T.lg[:, :, :], in_=lgr))
                ch.wait()
                ch.add(dve.reduce_max(out=T.mx[:, :], in_=T.lg[:, :, :], axis=AX))
                ch.wait()
                per_e = lambda a: a.rearrange("p (q a) -> p q a", a=1).broadcast_to([P, TILES, EXPERTS])
                dve.tensor_tensor(out=T.lg[:, :, :], in0=T.lg[:, :, :], in1=per_e(T.mx[:, :]),
                                  op=ALU.subtract).then_inc(T.lgr.sem, 1)
                dve.wait_ge(T.lgr.sem, T.lgr.at(i, 1))
                full = [P, TILES, EXPERTS, EXPERTS]
                lj = T.lg[:, :, :].rearrange("p q (a j) -> p q a j", a=1).broadcast_to(full)
                le = T.lg[:, :, :].rearrange("p q (e a) -> p q e a", a=1).broadcast_to(full)
                ch.add(dve.tensor_tensor(out=T.cmp[:, :, :, :], in0=lj, in1=le, op=ALU.is_gt))
                ch.add(dve.tensor_tensor(out=T.eq[:, :, :, :], in0=lj, in1=le, op=ALU.is_equal))
                ch.wait()
                low = earlier[:, :, :].rearrange("p (a e) j -> p a (e j)", a=1)\
                    .broadcast_to([P, TILES, EXPERTS * EXPERTS])
                eqf = T.eq[:, :, :, :].rearrange("p q e j -> p q (e j)")
                ch.add(dve.tensor_tensor(out=eqf, in0=eqf, in1=low, op=ALU.mult))
                ch.wait()
                ch.add(dve.tensor_tensor(out=T.cmp[:, :, :, :], in0=T.cmp[:, :, :, :], in1=T.eq[:, :, :, :],
                                         op=ALU.add))
                ch.wait()
                ch.add(dve.reduce_sum(out=T.rk[:, :, :], in_=T.cmp[:, :, :, :], axis=AX))
                ch.wait()
                dve.wait_ge(T.exr.sem, T.exr.at(i, 1))
                ch.add(dve.scalar_tensor_tensor(out=T.rk[:, :, :], in0=T.rk[:, :, :], scalar=1.5,
                                                in1=T.ex[:, :, :], op0=ALU.is_lt, op1=ALU.mult))
                ch.wait()
                ch.add(dve.reduce_sum(out=T.sm[:, :], in_=T.rk[:, :, :], axis=AX))
                ch.wait()
                ch.add(dve.reciprocal(out=T.sm[:, :], in_=T.sm[:, :]))
                ch.wait()
                ch.add(dve.tensor_tensor(out=T.eo[:, :, MOE:MOE + EXPERTS], in0=T.rk[:, :, :],
                                         in1=per_e(T.sm[:, :]), op=ALU.mult))
                ch.wait()
                for q in range(TILES):
                    dve.wait_ge(T.ye_ps.sem, T.ye_ps.at(i, q + 1))
                    y = T.po[q % 2][:, :].rearrange("p (e m) -> p e m", e=EXPERTS)
                    g = T.eo[:, q, MOE:MOE + EXPERTS].rearrange("p (e a) -> p e a", a=1)\
                        .broadcast_to([P, EXPERTS, MOE])
                    dve.tensor_tensor(out=T.gy[:, :, :], in0=y, in1=g, op=ALU.mult).then_inc(T.yer.sem, 1)
                    dve.wait_ge(T.yer.sem, T.yer.at(i, q + 1))
                    ins = dve.reduce_sum(out=T.eo[:, q, 0:MOE], in_=T.gy[:, :, :].rearrange("p e m -> p m e"),
                                         axis=AX)
                    if q < TILES - 1:
                        ch.add(ins)
                        ch.wait()
                    else:
                        ins.then_inc(T.eor.sem, 1)
                dve.wait_ge(T.dec_ps.sem, T.dec_ps.at(i, 1))
                bd = b_dec[:, :].rearrange("p (a d) -> p a d", a=1).broadcast_to([P, TILES, D])
                ch.add(dve.tensor_tensor(out=T.dd[:, :, :], in0=T.po[0][:, :].rearrange("p (q d) -> p q d", q=TILES),
                                         in1=bd, op=ALU.add))
                ch.wait()
                norm(T, ch, i, None, k + 1, T.dd, False, T.ddn)
                dve.wait_ge(T.ddg.sem, T.ddg.at(i, 1))
                dve.wait_ge(T.xpre.sem, T.xpre.at(i, l + 1))
                free()
                dve.tensor_tensor(out=dst[:, :, :], in0=T.xp[:, :, :], in1=T.dd[:, :, :],
                                  op=ALU.add).then_inc(dst_sem.sem, 1)

            def front(i):
                ch = Chain(dve, dve_f, DVE_F, i)
                ch.n = SET
                T = FR

                def first():
                    dve.wait_ge(x_in.sem, x_in.at(i, 16))

                ffn(ch, i, 0, 0, 0, xin, first)
                attn(ch, i)
                ffn(ch, i, 1, 2, 3, T.x, lambda: dve.wait_ge(T.x_new.sem, T.x_new.at(i, 2)))

                def free():
                    dve.wait_ge(BK.x_new.sem, BK.x_new.at(i, 0))

                moe(T, ch, i, 3, 5, BK.x, handed, free)
                assert ch.n - SET == DVE_F, ch.n - SET

            def back(i):
                ch = Chain(dve, dve_b, DVE_B, i)
                T = BK
                dve.wait_ge(handed.sem, handed.at(i, 1))
                norm(T, ch, i, 0, 0, T.x, False)
                dve.wait_ge(min_r.sem, min_r.at(i, IC))
                for c in range(IC):
                    ch.add(dve.tensor_scalar(out=cv[:, 0, c, :], in0=xc[:, c, 0:SEQ], scalar1=m_cw[:, c, 0:1],
                                             scalar2=m_cb[:, c:c + 1], op0=ALU.mult, op1=ALU.add))
                ch.wait()
                for c in range(IC):
                    ch.add(dve.scalar_tensor_tensor(out=cv[:, 1, c, :], in0=xc[:, c, 1:1 + SEQ],
                                                    scalar=m_cw[:, c, 1:2], in1=cv[:, 0, c, :],
                                                    op0=ALU.mult, op1=ALU.add))
                ch.wait()
                for c in range(IC):
                    ins = dve.scalar_tensor_tensor(out=cv[:, 0, c, :], in0=xc[:, c, 2:2 + SEQ],
                                                   scalar=m_cw[:, c, 2:3], in1=cv[:, 1, c, :],
                                                   op0=ALU.mult, op1=ALU.add)
                    if c < IC - 1:
                        ch.add(ins)
                    else:
                        ins.then_inc(cv_r.sem, 1)
                dve.wait_ge(cth_r.sem, cth_r.at(i, 1))
                dve.scalar_tensor_tensor(out=u2[:, :, :], in0=cth[:, :, :], scalar=1.0, in1=cv[:, 0, :, :],
                                         op0=ALU.add, op1=ALU.mult).then_inc(u2_r.sem, 1)
                dve.wait_ge(rth_r.sem, rth_r.at(i, 1))
                ch.add(dve.scalar_tensor_tensor(out=g4[:, :, :], in0=rth[:, :, :], scalar=1.0, in1=res[:, :, :],
                                                op0=ALU.add, op1=ALU.mult))
                dve.wait_ge(bcf_r.sem, bcf_r.at(i, 1))
                R = slice(64, 96)
                ch.add(dve.tensor_copy(out=bch[R, 0, :], in_=bc[R, 0, :]))
                ch.wait()
                ch.add(dve.tensor_tensor(out=bc[R, 1, :], in0=bc[R, 0, :], in1=bch[R, 0, :], op=ALU.subtract))
                dve.tensor_copy(out=bc3[0:32, :], in_=bch[R, 0, :]).then_inc(bc3_r.sem, 1)
                ch.wait()
                ch.add(dve.tensor_copy(out=bch[R, 1, :], in_=bc[R, 1, :]))
                ch.wait()
                dve.tensor_tensor(out=bc3[R, :], in0=bc[R, 1, :], in1=bch[R, 1, :],
                                  op=ALU.subtract).then_inc(bc3_r.sem, 1)
                dve.tensor_copy(out=bc3[32:64, :], in_=bch[R, 1, :]).then_inc(bc3_r.sem, 1)
                for c in range(IC):
                    dve.wait_ge(mabs_r.sem, mabs_r.at(i, c + 1))
                    dve.tensor_scalar(out=delta[:, c, :], in0=T.ps[c][:, :], scalar1=mb_dt[:, c:c + 1],
                                      scalar2=0.0, op0=ALU.add, op1=ALU.max).then_inc(mrelu_r.sem, 1)
                dve.wait_ge(mln_r.sem, mln_r.at(i, 1))
                dve.wait_ge(mrelu_r.sem, mrelu_r.at(i, IC))
                dve.tensor_tensor(out=delta[:, :, :], in0=delta[:, :, :], in1=dex[:, :, :],
                                  op=ALU.add).then_inc(delta_r.sem, 1)
                dve.wait_ge(delta_r.sem, delta_r.at(i, 1))
                dve.tensor_tensor(out=du[:, :, :], in0=delta[:, :, :], in1=u2[:, :, :],
                                  op=ALU.mult).then_inc(du_r.sem, 1)

                def read_out(n_):
                    b = n_ % 2
                    dve.wait_ge(cbc_ps.sem, cbc_ps.at(i, n_ + 1))
                    dve.wait_ge(hs_r.sem, hs_r.at(i, n_ + 1))
                    if n_ >= 2:
                        dve.wait_ge(sum_ps.sem, sum_ps.at(i, n_ - 1))
                    c_n = T.ps[1][:, :].rearrange("p (a t) -> p a t", a=1).broadcast_to([P, IC, SEQ])
                    v = lambda a: a.rearrange("p (c t) -> p c t", c=IC)
                    dve.tensor_tensor(out=v(hc[:, b, :]), in0=v(hs[:, b, :]), in1=c_n,
                                      op=ALU.mult).then_inc(hc_r.sem, 1)

                for n_ in range(STATES):
                    b = n_ % 2
                    dve.wait_ge(dA_r.sem, dA_r.at(i, n_ + 1))
                    dve.wait_ge(dbu_r.sem, dbu_r.at(i, n_ + 1))
                    if n_ >= 2:
                        dve.wait_ge(hc_r.sem, hc_r.at(i, n_ - 1))
                    dve.tensor_tensor_scan(out=hs[:, b, :], data0=dA[:, b, :], data1=dbu[:, b, :],
                                           initial=0.0, op0=ALU.mult, op1=ALU.add).then_inc(hs_r.sem, 1)
                    if n_ >= 1:
                        read_out(n_ - 1)
                read_out(STATES - 1)
                dve.wait_ge(sum_ps.sem, sum_ps.at(i, STATES))
                for c in range(IC):
                    ins = dve.tensor_tensor(out=yg[:, c, :], in0=T.po[c][:, :], in1=g4[:, c, :], op=ALU.mult)
                    if c < IC - 1:
                        ch.add(ins)
                    else:
                        ins.then_inc(yg_r.sem, 1)
                dve.wait_ge(mo_ps.sem, mo_ps.at(i, 1))
                dve.wait_ge(T.xpre.sem, T.xpre.at(i, 1))
                dve.tensor_tensor(out=T.x[:, :, :], in0=T.ps[0][:, :].rearrange("p (q d) -> p q d", q=TILES),
                                  in1=T.xp[:, :, :], op=ALU.add).then_inc(T.x_new.sem, 1)

                def free():
                    dve.wait_ge(xo_free.sem, xo_free.at(i, 0))

                moe(T, ch, i, 1, 1, xo, T.x_new, free)
                assert ch.n == DVE_B, ch.n

            with dve.Fori(0, BATCH) as i:
                front(i)
                back(i)

        @block.scalar
        def _(act):
            act.wait_ge(loads, 16 * N_LOADS)
            act.activation(out=tmp[:, :], in_=w1[:, :], func=ACT.Abs, accum_out=qs[:, 2:3]).then_inc(act_setup, 1)
            act.wait_ge(act_setup, 1)
            act.activation(out=tmp[:, :], in_=tmp2[:, :], func=ACT.Abs, accum_out=qs[:, 6:7]).then_inc(act_setup, 1)
            act.preload_act_table_set("natural_log_exp_and_others")
            act.activation(out=mA[:, :, :], in_=mA[:, :, :], func=ACT.Exp).then_inc(act_setup, 1)
            act.activation(out=aA[:, :], in_=aA[:, :], func=ACT.Exp).then_inc(act_setup, 1)
            act.wait_ge(dve_setup, 2)

            def zt(T, i, l):
                act.wait_ge(T.zt_ps.sem, T.zt_ps.at(i, l + 1))
                act.activation(out=T.zT[:, :], in_=T.ps[0][:, :], func=ACT.Copy).then_inc(T.zt.sem, 1)

            def ffn(i, f, l):
                act.preload_act_table(ACT.Gelu)
                zt(FR, i, l)
                for c in range(HC):
                    act.wait_ge(h_ps.sem, h_ps.at(i, f * HC + c + 1))
                    act.activation(out=hT[:, c, :], in_=FR.ps[(c + 1) % 2][:, :], func=ACT.Gelu,
                                   bias=b1[:, c:c + 1]).then_inc(h_r.sem, 1)

            def attn(i):
                T = FR
                R = slice(64, 64 + STATES)
                zt(T, i, 1)
                act.wait_ge(az_ps.sem, az_ps.at(i, 1))
                act.activation(out=gz[:, :], in_=T.ps[1][:, :], func=ACT.Gelu, bias=ab_z[:, :]).then_inc(gz_r.sem, 1)
                act.preload_act_table_set("natural_log_exp_and_others")
                act.wait_ge(as_ps.sem, as_ps.at(i, 1))
                act.activation(out=bcd[:, :], in_=T.ps[0][0:96, :], func=ACT.Identity,
                               bias=ab_s[:, :]).then_inc(bcd_r.sem, 1)
                ch = Chain(act, act_f, ACT_F, i)
                act.wait_ge(bcd_r.sem, bcd_r.at(i, 1))
                ch.add(act.activation(out=adt[R, 0, :], in_=bcd[R, :], func=ACT.Abs))
                ch.wait()
                ch.add(act.activation(out=adt[R, 0, :], in_=adt[R, 0, :], func=ACT.Exp, scale=-1.0))
                ch.wait()
                act.activation(out=adt[R, 1, :], in_=adt[R, 0, :], func=ACT.Ln, bias=1.0).then_inc(aln_r.sem, 1)
                act.wait_ge(adelta_r.sem, adelta_r.at(i, 1))
                act.activation(out=adA[:, :], in_=adt[R, 2, :], func=ACT.Exp,
                               scale=aA[R, :]).then_inc(adA_r.sem, 1)
                assert ch.n == ACT_F

            def moe(T, i, l):
                act.preload_act_table(ACT.Exp)
                zt(T, i, l)
                for c in range(EC):
                    act.wait_ge(T.enc_ps.sem, T.enc_ps.at(i, c + 1))
                    act.activation(out=T.s1[:, c, :], in_=T.ps[(c + 1) % 2][:, :], func=ACT.Tanh,
                                   bias=b_enc[:, c:c + 1], scale=0.5).then_inc(T.s1r.sem, 1)
                for e in range(EXPERTS):
                    act.wait_ge(T.he_ps.sem, T.he_ps.at(i, e + 1))
                    act.activation(out=T.he[:, e, :], in_=T.ps[(e + 1) % 2][:, :],
                                   func=ACT.Relu).then_inc(T.her.sem, 1)
                    if e == 3:
                        act.wait_ge(T.lgr.sem, T.lgr.at(i, 1))
                        act.activation(out=T.ex[:, :, :], in_=T.lg[:, :, :], func=ACT.Exp).then_inc(T.exr.sem, 1)
                act.wait_ge(T.eoT_ps.sem, T.eoT_ps.at(i, 1))
                act.activation(out=T.eoT[:, :], in_=T.ps[0][0:MOE + EXPERTS, :],
                               func=ACT.Copy).then_inc(T.eoTr.sem, 1)
                for c in range(EC):
                    act.wait_ge(T.c2s_ps.sem, T.c2s_ps.at(i, c + 1))
                    act.activation(out=T.s1[:, c, :], in_=T.ps[(c + 1) % 2][:, :], func=ACT.Tanh,
                                   bias=b_c2s[:, c:c + 1], scale=0.5).then_inc(T.s2r.sem, 1)

            def front(i):
                ffn(i, 0, 0)
                attn(i)
                ffn(i, 1, 2)
                moe(FR, i, 3)

            def back(i):
                T = BK
                zt(T, i, 0)
                for c in range(2 * IC):
                    act.wait_ge(min_ps.sem, min_ps.at(i, c + 1))
                    dst = xc[:, c, TAPS - 1:] if c < IC else res[:, c - IC, :]
                    act.activation(out=dst, in_=T.ps[(c + 1) % 2][:, :], func=ACT.Identity,
                                   bias=mb_in[:, c:c + 1]).then_inc(min_r.sem, 1)
                act.wait_ge(cv_r.sem, cv_r.at(i, 1))
                act.activation(out=cth[:, :, :], in_=cv[:, 0, :, :], func=ACT.Tanh, scale=0.5).then_inc(cth_r.sem, 1)
                act.wait_ge(min_r.sem, min_r.at(i, 2 * IC))
                act.activation(out=rth[:, :, :], in_=res[:, :, :], func=ACT.Tanh, scale=0.5).then_inc(rth_r.sem, 1)
                act.preload_act_table_set("natural_log_exp_and_others")
                act.wait_ge(mx_ps.sem, mx_ps.at(i, 1))
                act.activation(out=dlt[:, :], in_=T.ps[1][0:RANK, :], func=ACT.Copy).then_inc(dlt_r.sem, 1)
                act.activation(out=bc[64:96, 0, :], in_=T.ps[1][64:96, :], func=ACT.Copy).then_inc(bcf_r.sem, 1)
                for c in range(IC):
                    act.wait_ge(mdt_ps.sem, mdt_ps.at(i, c + 1))
                    act.activation(out=dab[:, c, :], in_=T.ps[c][:, :], func=ACT.Abs,
                                   bias=mb_dt[:, c:c + 1]).then_inc(mabs_r.sem, 1)
                ch = Chain(act, act_b, ACT_B, i)
                act.wait_ge(mabs_r.sem, mabs_r.at(i, IC))
                ch.add(act.activation(out=dab[:, :, :], in_=dab[:, :, :], func=ACT.Exp, scale=-1.0))
                ch.wait()
                act.activation(out=dex[:, :, :], in_=dab[:, :, :], func=ACT.Ln, bias=1.0).then_inc(mln_r.sem, 1)
                act.wait_ge(delta_r.sem, delta_r.at(i, 1))
                for n_ in range(STATES):
                    b = n_ % 2
                    act.wait_ge(bbc_ps.sem, bbc_ps.at(i, n_ + 1))
                    if n_ >= 2:
                        act.wait_ge(dbu_r.sem, dbu_r.at(i, n_ - 1))
                    act.activation(out=bbc[:, b, :], in_=T.ps[0][:, :], func=ACT.Copy).then_inc(bbc_r.sem, 1)
                    if n_ >= 2:
                        act.wait_ge(hs_r.sem, hs_r.at(i, n_ - 1))
                    for c in range(IC):
                        dst = dA[:, b, c * SEQ:(c + 1) * SEQ].rearrange("p (k t) -> p k t", t=CHUNK)[:, :, 1:]
                        src = delta[:, c, :].rearrange("p (k t) -> p k t", t=CHUNK)[:, :, 1:]
                        ins = act.activation(out=dst, in_=src, func=ACT.Exp, scale=mA[:, c, n_:n_ + 1])
                        if c < IC - 1:
                            ch.add(ins)
                        else:
                            ins.then_inc(dA_r.sem, 1)
                assert ch.n == ACT_B, ch.n
                moe(T, i, 1)

            with act.Fori(0, BATCH) as i:
                front(i)
                back(i)

        @block.tensor
        def _(pe):
            pe.wait_ge(pool_const, 2)
            for k in range(2):
                pe.wait_ge(act_setup, k + 1)
                pe.matmul(FR.ps[k][:, 0:1], lhsT=ones[:, :], rhs=qs[:, 4 * k + 2:4 * k + 3],
                          start=True, stop=True).then_inc(pe_setup, 1)
            pe.wait_ge(dve_setup, 1)

            def total(dst, lhs, rhs, m):
                for c in range(m):
                    last = pe.matmul(dst, lhsT=lhs(c), rhs=rhs(c), start=(c == 0), stop=(c == m - 1))
                return last
            total(FR.po[0][:, 0:P], lambda c: mean512[:, :], lambda c: w2[:, c, 0:P], HC)
            total(FR.po[0][:, P:2 * P], lambda c: ones[:, :], lambda c: tmp[:, c * P:(c + 1) * P], HC)
            for j in range(HC):
                pe.matmul(FR.po[0][:, 2 * P + j:2 * P + j + 1], lhsT=w1q[:, j * P:(j + 1) * P], rhs=ln1b[:, :],
                          start=True, stop=True)
            total(FR.po[1][:, 0:P], lambda c: ones[:, :], lambda c: w_dec[:, c, :], EC)
            total(FR.po[1][0:MOE, P:P + 1], lambda c: w_s2c[:, c, :], lambda c: ones[:, 0:1], EC)
            pe.matmul(FR.ps[1][0:EXPERTS, 0:ENC], lhsT=b_e2[:, :], rhs=w_c2s[0:MOE, :],
                      start=True, stop=True).then_inc(pe_setup, 1)
            pe.wait_ge(dve_setup, 2)

            def zt(T, i, l):
                for q in range(TILES):
                    pe.wait_ge(T.zn.sem, T.zn.at(i, l * TILES + q + 1))
                    last = pe.transpose(T.ps[0][:, q * P:(q + 1) * P], in_=T.z[:, q, :], identity=ident[:, :])
                last.then_inc(T.zt_ps.sem, 1)
                pe.wait_ge(T.zt.sem, T.zt.at(i, l + 1))

            def ffn(i, f, l):
                T = FR
                zt(T, i, l)
                for c in range(HC):
                    if c >= 2:
                        pe.wait_ge(h_r.sem, h_r.at(i, f * HC + c - 1))
                    pe.matmul(T.ps[(c + 1) % 2][:, :], lhsT=w1[:, c * P:(c + 1) * P], rhs=T.zT[:, :],
                              start=True, stop=True).then_inc(h_ps.sem, 1)
                pe.wait_ge(h_r.sem, h_r.at(i, f * HC + HC))
                pe.wait_ge(sq_r.sem, sq_r.at(i, f * HC + HC))
                for q in range(TILES):
                    o = T.po[q // 2][:, (q % 2) * 256:(q % 2) * 256 + P + 2]
                    for c in range(HC):
                        pe.matmul(o[:, 0:P + 1], lhsT=hT[:, c, q * P:(q + 1) * P], rhs=w2[:, c, 0:P + 1],
                                  start=(c == 0), stop=(c == HC - 1))
                    for c in range(HC):
                        last = pe.matmul(o[:, P + 1:P + 2], lhsT=sq[:, c, q * P:(q + 1) * P],
                                         rhs=w2[:, c, P + 1:P + 2], start=(c == 0), stop=(c == HC - 1))
                last.then_inc(fo_ps.sem, 1)

            def attn(i):
                T = FR
                zt(T, i, 1)
                pe.matmul(T.ps[1][:, :], lhsT=aw_z[:, :], rhs=T.zT[:, :], start=True, stop=True).then_inc(az_ps.sem, 1)
                pe.matmul(T.ps[0][0:96, :], lhsT=aw_s[:, :], rhs=T.zT[:, :], start=True,
                          stop=True).then_inc(as_ps.sem, 1)
                pe.wait_ge(gz_r.sem, gz_r.at(i, 1))
                for q in range(TILES):
                    pe.matmul(T.po[0][:, q * P:(q + 1) * P], lhsT=gz[:, q * P:(q + 1) * P], rhs=aw_o[:, :],
                              start=True, stop=True)
                pe.wait_ge(ap_r.sem, ap_r.at(i, 1))
                for q in range(TILES):
                    last = pe.matmul(T.po[1][:, q:q + 1], lhsT=ap_[32:32 + STATES, q * P:(q + 1) * P],
                                     rhs=ones[32:32 + STATES, 0:1], start=True, stop=True)
                last.then_inc(ao_ps.sem, 1)

            def moe(T, i, l):
                zt(T, i, l)
                for c in range(EC):
                    pe.matmul(T.ps[(c + 1) % 2][:, :], lhsT=w_enc[:, c * P:(c + 1) * P], rhs=T.zT[:, :],
                              start=True, stop=True).then_inc(T.enc_ps.sem, 1)
                pe.wait_ge(T.s1r.sem, T.s1r.at(i, EC))
                for c in range(EC):
                    last = pe.matmul(T.ps[0][0:MOE, :], lhsT=w_s2c[:, c, :], rhs=T.s1[:, c, :],
                                     start=(c == 0), stop=(c == EC - 1))
                last.then_inc(T.cont_ps.sem, 1)
                pe.wait_ge(T.contr.sem, T.contr.at(i, 1))
                for q in range(TILES):
                    last = pe.matmul(T.po[0][:, q * EXPERTS:(q + 1) * EXPERTS],
                                     lhsT=T.cont[:, q * P:(q + 1) * P], rhs=w_r[:, :], start=True, stop=True)
                last.then_inc(T.route_ps.sem, 1)
                for e in range(EXPERTS):
                    if e >= 2:
                        pe.wait_ge(T.her.sem, T.her.at(i, e - 1))
                    pe.matmul(T.ps[(e + 1) % 2][:, :], lhsT=w_e1[:, e, :], rhs=T.cont[:, :],
                              start=True, stop=True).then_inc(T.he_ps.sem, 1)
                pe.wait_ge(T.her.sem, T.her.at(i, EXPERTS))
                pe.wait_ge(T.lgr.sem, T.lgr.at(i, 1))
                for q in range(TILES):
                    if q >= 2:
                        pe.wait_ge(T.yer.sem, T.yer.at(i, q - 1))
                    for e in range(EXPERTS):
                        last = pe.matmul(T.po[q % 2][:, e * MOE:(e + 1) * MOE],
                                         lhsT=T.he[:, e, q * P:(q + 1) * P], rhs=w_e2[:, e, :],
                                         start=True, stop=True)
                    last.then_inc(T.ye_ps.sem, 1)
                pe.wait_ge(T.eor.sem, T.eor.at(i, 1))
                for q in range(TILES):
                    last = pe.transpose(T.ps[0][0:MOE + EXPERTS, q * P:(q + 1) * P], in_=T.eo[:, q, :],
                                        identity=ident[:, :])
                last.then_inc(T.eoT_ps.sem, 1)
                pe.wait_ge(T.eoTr.sem, T.eoTr.at(i, 1))
                for c in range(EC):
                    pe.matmul(T.ps[(c + 1) % 2][:, :], lhsT=w_c2s[:, c * P:(c + 1) * P], rhs=T.eoT[:, :],
                              start=True, stop=True).then_inc(T.c2s_ps.sem, 1)
                pe.wait_ge(T.s2r.sem, T.s2r.at(i, EC))
                for q in range(TILES):
                    for c in range(EC):
                        last = pe.matmul(T.po[0][:, q * P:(q + 1) * P], lhsT=T.s1[:, c, q * P:(q + 1) * P],
                                         rhs=w_dec[:, c, :], start=(c == 0), stop=(c == EC - 1))
                last.then_inc(T.dec_ps.sem, 1)

            def front(i):
                ffn(i, 0, 0)
                attn(i)
                ffn(i, 1, 2)
                moe(FR, i, 3)

            def back(i):
                T = BK
                zt(T, i, 0)
                for c in range(2 * IC):
                    if c >= 2:
                        pe.wait_ge(min_r.sem, min_r.at(i, c - 1))
                    pe.matmul(T.ps[(c + 1) % 2][:, :], lhsT=mw_in[:, c * P:(c + 1) * P], rhs=T.zT[:, :],
                              start=True, stop=True).then_inc(min_ps.sem, 1)
                pe.wait_ge(min_r.sem, min_r.at(i, 2 * IC))
                pe.wait_ge(u2_r.sem, u2_r.at(i, 1))
                for c in range(IC):
                    last = pe.matmul(T.ps[1][0:96, :], lhsT=mw_x[:, c, :], rhs=u2[:, c, :],
                                     start=(c == 0), stop=(c == IC - 1))
                last.then_inc(mx_ps.sem, 1)
                pe.wait_ge(dlt_r.sem, dlt_r.at(i, 1))
                pe.wait_ge(bcf_r.sem, bcf_r.at(i, 1))
                for c in range(IC):
                    pe.matmul(T.ps[c][:, :], lhsT=mw_dt[:, c * P:(c + 1) * P], rhs=dlt[:, :],
                              start=True, stop=True).then_inc(mdt_ps.sem, 1)
                pe.wait_ge(bc3_r.sem, bc3_r.at(i, 3))
                pe.wait_ge(mrelu_r.sem, mrelu_r.at(i, IC))

                def add_up(n_):
                    pe.wait_ge(hc_r.sem, hc_r.at(i, n_ + 1))
                    for c in range(IC):
                        last = pe.matmul(T.po[c][:, :], lhsT=ident[:, :], rhs=hc[:, n_ % 2, c * SEQ:(c + 1) * SEQ],
                                         start=(n_ == 0), stop=(n_ == STATES - 1))
                    last.then_inc(sum_ps.sem, 1)

                for n_ in range(STATES):
                    if n_ >= 1:
                        pe.wait_ge(bbc_r.sem, bbc_r.at(i, n_))
                    pe.matmul(T.ps[0][:, :], lhsT=sel[:, n_, :], rhs=bc3[:, :], start=True,
                              stop=True).then_inc(bbc_ps.sem, 1)
                    if n_ >= 1:
                        pe.wait_ge(hc_r.sem, hc_r.at(i, n_))
                    pe.matmul(T.ps[1][:, :], lhsT=sel[:, STATES + n_, :], rhs=bc3[:, :], start=True,
                              stop=True).then_inc(cbc_ps.sem, 1)
                    if n_ >= 1:
                        add_up(n_ - 1)
                add_up(STATES - 1)
                pe.wait_ge(yg_r.sem, yg_r.at(i, 1))
                for q in range(TILES):
                    for c in range(IC):
                        last = pe.matmul(T.ps[0][:, q * P:(q + 1) * P], lhsT=yg[:, c, q * P:(q + 1) * P],
                                         rhs=mw_o[:, c, :], start=(c == 0), stop=(c == IC - 1))
                last.then_inc(mo_ps.sem, 1)
                pe.wait_ge(T.x_new.sem, T.x_new.at(i, 1))
                moe(T, i, 1)

            with pe.Fori(0, BATCH) as i:
                front(i)
                back(i)


N_LOADS = 31 + 7
COLUMNS = {"L0_ffn_ln2_g": HC, "L0_ffn_ln2_b": HC, "L0_ffn_b1": HC, "L1_ffn_b_enc": EC, "L1_ffn_b_c2s": EC,
           "L1_attn_b_in": 2 * IC, "L1_attn_conv_b": IC, "L1_attn_b_dt": IC}
COLUMNS_AT = [sum(list(COLUMNS.values())[:k]) for k in range(len(COLUMNS))]
N_COLUMNS = sum(COLUMNS.values())
DVE_F, DVE_B = 79, 52
ACT_F, ACT_B = 2, 1 + STATES


def kernel(**inputs):
    import concourse.bacc as bacc
    from concourse.bass_utils import run_bass_kernel_spmd

    a = {k: np.ascontiguousarray(v) for k, v in inputs.items()}
    a["columns"] = np.ascontiguousarray(np.concatenate([a.pop(k).reshape(-1, P).T for k in COLUMNS], axis=1))
    w2 = np.asarray(a["L0_ffn_w2"])
    a["w1T"] = np.ascontiguousarray(a.pop("L0_ffn_w1").T)
    a["w2T"] = np.ascontiguousarray(w2.T.reshape(HC, P, D).transpose(1, 0, 2).reshape(P, HC * D))
    a.pop("L0_ffn_w2")
    a["moe_b2T"] = np.ascontiguousarray(a.pop("L1_ffn_b2").T)
    a["mamba_W_inT"] = np.ascontiguousarray(a.pop("L1_attn_W_in").T)
    a["mamba_W_xT"] = np.ascontiguousarray(a.pop("L1_attn_W_x").T)
    a["mamba_W_dtT"] = np.ascontiguousarray(a.pop("L1_attn_W_dt").T)
    a["mamba_W_outT"] = np.ascontiguousarray(a.pop("L1_attn_W_out").T)
    nc = bacc.Bacc("TRN2", target_bir_lowering=False, num_devices=1)
    A = {k: nc.dram_tensor(k, v.shape, F32, kind="ExternalInput").ap() for k, v in a.items()}
    out = nc.dram_tensor("out", (BATCH, SEQ, D), F32, kind="ExternalOutput").ap()
    build(nc, A, out)
    r = run_bass_kernel_spmd(nc, [a], core_ids=[0])
    return r.results[0]["out"]
```

```python
import numpy as np
import concourse.bass as bass
from concourse import mybir
from contextlib import ExitStack

BATCH, SEQ, D = 8, 512, 128
P = 128
TILES = SEQ // P
HIDDEN = 512
HC = HIDDEN // P
STATES = 16
ENC = 256
EC = ENC // P
MOE = 64
EXPERTS = 8
EH = 128
INNER = 256
IC = INNER // P
RANK = 64
CHUNK = 32
TAPS = 3
EPS = 1e-5

F32 = mybir.dt.float32
BF16 = mybir.dt.bfloat16
ALU = mybir.AluOpType
ACT = mybir.ActivationFunctionType
AX = mybir.AxisListType.X


def first(i):
    return isinstance(i, int) and i == 0


class Signal:

    def __init__(self, sem, per, start=0):
        self.sem, self.per, self.start = sem, per, start

    def at(self, i, n):
        return i * self.per + n + self.start


class Chain:

    def __init__(self, eng, sem, per, i):
        self.eng, self.sem, self.per, self.i, self.n = eng, sem, per, i, 0

    def add(self, ins):
        ins.then_inc(self.sem, 1)
        self.n += 1

    def wait(self):
        self.eng.wait_ge(self.sem, self.i * self.per + self.n)


FFN = 0
ATTN = 6
FFN_2 = 11
MOE_F = 17
FRONT_END = 32
MAMBA = 0
SCAN = 7
MAMBA_OUT = SCAN + STATES + 1
MOE_B = MAMBA_OUT + 2
BACK_END = MOE_B + 15
SCHEDULE = [(round((k + 1) * FRONT_END / BACK_END), k) for k in range(BACK_END)]


def alone(steps):
    for _ in steps:
        pass


def side_by_side(front, back):
    f, b = next(front, None), next(back, None)
    for f_last, b_last in SCHEDULE:
        while b is not None and b <= b_last:
            b = next(back, None)
        while f is not None and f <= f_last:
            f = next(front, None)
    assert f is None and b is None


def build(nc, A, out):
    ctx = ExitStack()
    with ctx:
        def sb(name, shape, dt=F32):
            return ctx.enter_context(nc.sbuf_tensor(name, shape, dt))

        def pb(name, shape, dt=F32):
            return ctx.enter_context(nc.psum_tensor(name, shape, dt))

        def sem(name):
            return ctx.enter_context(nc.semaphore(name))

        ident = sb("ident", [P, P])
        ones = sb("ones", [P, P])
        mean512 = sb("mean512", [P, P])
        neg_half = sb("neg_half", [P, TILES])
        earlier = sb("earlier", [P, EXPERTS, EXPERTS])
        sel = sb("sel", [96, 2 * STATES, P], BF16)
        columns = sb("vectors", [P, N_COLUMNS])
        ln2g, ln2b, b1, b_enc, b_c2s, mb_in, m_cb, mb_dt = (
            columns[:, at:at + n] for at, n in zip(COLUMNS_AT, COLUMNS.values()))
        w1 = sb("w1", [P, HIDDEN])
        w2 = sb("w2", [P, HC, P + 2])
        qs = sb("qs", [P, 8])
        ln1g = sb("ln1g", [P, 1])
        ln1b = sb("ln1b", [P, 1])
        bias2 = sb("bias2", [P, D])
        aw_z = sb("aw_z", [P, D])
        aw_s = sb("aw_s", [P, 96])
        ab_z = sb("ab_z", [P, 1])
        ab_s = sb("ab_s", [96, 1])
        aA = sb("aA", [96, 1])
        aw_o = sb("aw_o", [P, D])
        ab_o = sb("ab_o", [P, D])
        w_enc = sb("w_enc", [P, ENC])
        w_s2c = sb("w_s2c", [P, EC, MOE])
        b_s2c = sb("b_s2c", [MOE, 1])
        w_r = sb("w_r", [MOE + 1, EXPERTS])
        w_e1 = sb("w_e1", [MOE + 1, EXPERTS, EH])
        w_e2 = sb("w_e2", [P, EXPERTS, MOE])
        b_e2 = sb("b_e2", [MOE, EXPERTS])
        w_c2s = sb("w_c2s", [MOE + EXPERTS, ENC])
        w_dec = sb("w_dec", [P, EC, D])
        b_dec = sb("b_dec", [P, D])
        mlng = sb("mlng", [P, D])
        mlnb = sb("mlnb", [P, D])
        mw_in = sb("mw_in", [P, 2 * INNER])
        m_cw = sb("m_cw", [P, IC, TAPS])
        mw_x = sb("mw_x", [P, IC, RANK + 2 * STATES])
        mw_dt = sb("mw_dt", [RANK, INNER])
        mA = sb("mA", [P, IC, STATES])
        mw_o = sb("mw_o", [P, IC, D])
        mb_o = sb("mb_o", [P, D])

        loads = sem("loads")
        iota_done = sem("iota_done")
        pool_const = sem("pool_const")
        dve_setup = sem("dve_setup")
        act_setup = sem("act_setup")
        pe_setup = sem("pe_setup")

        class Thread:

            def __init__(self, n, lns, moes, ffns, updates, wide):
                self.n = n
                self.he = wide
                self.x = sb(n + "x", [P, TILES, D])
                self.xp = sb(n + "xp", [P, TILES, D])
                self.st = sb(n + "st", [P, TILES, 6])
                self.mv = sb(n + "mv", [P, TILES, 2])
                self.vv = sb(n + "vv", [P, TILES])
                self.rs = sb(n + "rs", [P, TILES])
                self.z = sb(n + "z", [P, TILES, D])
                self.zT = sb(n + "zT", [P, SEQ])
                self.ps = [pb(f"{n}ps{k}", [P, 512]) for k in range(2)]
                self.po = [pb(f"{n}po{k}", [P, 512]) for k in range(2)]
                norms = lns + moes + ffns
                self.var = Signal(sem(n + "var"), norms)
                self.rstd = Signal(sem(n + "rstd"), norms)
                self.xpre = Signal(sem(n + "xpre"), lns)
                self.x_new = Signal(sem(n + "x_new"), updates, 1)
                self.zn = Signal(sem(n + "zn"), lns * TILES)
                self.zt_ps = Signal(sem(n + "zt_ps"), lns)
                self.zt = Signal(sem(n + "zt"), lns)
                self.s1 = sb(n + "s1", [P, EC, SEQ])
                self.cont = sb(n + "cont", [MOE + 1, SEQ])
                self.lg = sb(n + "lg", [P, TILES, EXPERTS])
                self.mx = sb(n + "mx", [P, TILES])
                self.ex = sb(n + "ex", [P, TILES, EXPERTS])
                self.cmp = sb(n + "cmp", [P, TILES, EXPERTS, EXPERTS])
                self.eq = sb(n + "eq", [P, TILES, EXPERTS, EXPERTS])
                self.rk = sb(n + "rk", [P, TILES, EXPERTS])
                self.sm = sb(n + "sm", [P, TILES])
                self.eo = sb(n + "eo", [P, TILES, MOE + EXPERTS])
                self.gy = sb(n + "gy", [P, EXPERTS, MOE])
                self.eoT = sb(n + "eoT", [MOE + EXPERTS, SEQ])
                self.dd = sb(n + "dd", [P, TILES, D])
                self.enc_ps = Signal(sem(n + "enc_ps"), moes * EC)
                self.s1r = Signal(sem(n + "s1r"), moes * EC)
                self.cont_ps = Signal(sem(n + "cont_ps"), moes)
                self.contr = Signal(sem(n + "contr"), moes)
                self.route_ps = Signal(sem(n + "route_ps"), moes)
                self.lgr = Signal(sem(n + "lgr"), moes)
                self.exr = Signal(sem(n + "exr"), moes)
                self.he_ps = Signal(sem(n + "he_ps"), moes * EXPERTS)
                self.her = Signal(sem(n + "her"), moes * EXPERTS)
                self.ye_ps = Signal(sem(n + "ye_ps"), moes * TILES)
                self.yer = Signal(sem(n + "yer"), moes * TILES)
                self.eor = Signal(sem(n + "eor"), moes)
                self.eoT_ps = Signal(sem(n + "eoT_ps"), moes)
                self.eoTr = Signal(sem(n + "eoTr"), moes)
                self.c2s_ps = Signal(sem(n + "c2s_ps"), moes * EC)
                self.s2r = Signal(sem(n + "s2r"), moes * EC)
                self.dec_ps = Signal(sem(n + "dec_ps"), moes)
                self.ddn = Signal(sem(n + "ddn"), moes)
                self.ddg = Signal(sem(n + "ddg"), moes)

        fwide = sb("fwide", [P, EXPERTS, SEQ])
        bwide = sb("bwide", [P, EXPERTS, SEQ])
        FR = Thread("f_", 4, 1, 2, 3, fwide)
        BK = Thread("b_", 2, 1, 0, 2, bwide)
        w1q, tmp, tmp2 = FR.s1[:, 0, :], BK.s1[:, 0, :], BK.s1[:, 1, :]
        w2q = FR.s1[:, 1, :].rearrange("p (c d) -> p c d", c=HC)
        xin = sb("xin", [P, TILES, D])
        hT = fwide[:, 0:HC, :]
        sq = fwide[:, HC:2 * HC, :]
        fs = sb("fs", [P, 2, 2, 2])
        fvar = sb("fvar", [P, TILES])
        frs = sb("frs", [P, TILES])
        gz = sb("gz", [P, SEQ])
        bcd = sb("bcd", [96, SEQ])
        adt = sb("adt", [96, 3, SEQ])
        adA = sb("adA", [STATES, SEQ])
        ah = sb("ah", [64, SEQ])
        ap_ = sb("ap_", [64, SEQ])
        ay = sb("ay", [P, TILES])
        x_in = Signal(sem("x_in"), 16)
        h_ps = Signal(sem("h_ps"), 2 * HC)
        h_r = Signal(sem("h_r"), 2 * HC)
        sq_r = Signal(sem("sq_r"), 2 * HC)
        fo_ps = Signal(sem("fo_ps"), 2)
        az_ps = Signal(sem("az_ps"), 1)
        as_ps = Signal(sem("as_ps"), 1)
        bcd_r = Signal(sem("bcd_r"), 1)
        gz_r = Signal(sem("gz_r"), 1)
        aln_r = Signal(sem("aln_r"), 1)
        adelta_r = Signal(sem("adelta_r"), 1)
        adA_r = Signal(sem("adA_r"), 1)
        ap_r = Signal(sem("ap_r"), 1)
        ao_ps = Signal(sem("ao_ps"), 1)
        xc = sb("xc", [P, IC, SEQ + TAPS - 1])
        res = sb("res", [P, IC, SEQ])
        rth = sb("rth", [P, IC, SEQ])
        cv = sb("cv", [P, 2, IC, SEQ])
        u2 = sb("u2", [P, IC, SEQ])
        g4 = sb("g4", [P, IC, SEQ])
        dlt = sb("dlt", [RANK, SEQ])
        bc = sb("bc", [96, 3, SEQ])
        bch = sb("bch", [96, 2, SEQ], BF16)
        bc3 = sb("bc3", [96, SEQ], BF16)
        dab = sb("dab", [P, IC, SEQ])
        dex = sb("dex", [P, IC, SEQ])
        cth = dex
        delta = sb("delta", [P, IC, SEQ])
        du = cv[:, 1, :, :]
        dA = sb("dA", [P, 2, IC * SEQ])
        bbc = sb("bbc", [P, 2, SEQ])
        dbu = sb("dbu", [P, 2, IC * SEQ])
        hs = bwide[:, 0:4, :].rearrange("p (b c) t -> p b (c t)", b=2)
        hc = bwide[:, 4:8, :].rearrange("p (b c) t -> p b (c t)", b=2)
        yg = u2
        xo = sb("xo", [P, TILES, D])
        hx = sb("hx", [P, TILES, D])
        handed = Signal(sem("handed"), 1)
        min_ps = Signal(sem("min_ps"), 2 * IC)
        min_r = Signal(sem("min_r"), 2 * IC)
        rth_r = Signal(sem("rth_r"), 1)
        cv_r = Signal(sem("cv_r"), 1)
        cth_r = Signal(sem("cth_r"), 1)
        u2_r = Signal(sem("u2_r"), 1)
        mx_ps = Signal(sem("mx_ps"), 1)
        dlt_r = Signal(sem("dlt_r"), 1)
        bcf_r = Signal(sem("bcf_r"), 1)
        bc3_r = Signal(sem("bc3_r"), 3)
        mdt_ps = Signal(sem("mdt_ps"), IC)
        mrelu_r = Signal(sem("mrelu_r"), IC)
        mabs_r = Signal(sem("mabs_r"), IC)
        mln_r = Signal(sem("mln_r"), 1)
        delta_r = Signal(sem("delta_r"), 1)
        du_r = Signal(sem("du_r"), 1)
        dA_r = Signal(sem("dA_r"), STATES)
        bbc_ps = Signal(sem("bbc_ps"), STATES)
        bbc_r = Signal(sem("bbc_r"), STATES)
        cbc_ps = Signal(sem("cbc_ps"), STATES)
        dbu_r = Signal(sem("dbu_r"), STATES)
        hs_r = Signal(sem("hs_r"), STATES)
        hc_r = Signal(sem("hc_r"), STATES)
        sum_ps = Signal(sem("sum_ps"), STATES)
        yg_r = Signal(sem("yg_r"), 1)
        mo_ps = Signal(sem("mo_ps"), 1)
        xo_free = Signal(sem("xo_free"), 16, 1)
        dve_f, dve_b = sem("dve_f"), sem("dve_b")
        act_f, act_b = sem("act_f"), sem("act_b")

        block = ctx.enter_context(nc.Block())
        row = lambda ap: ap.rearrange("(a n) -> a n", a=1)
        col = lambda ap: ap.rearrange("(p a) -> p a", a=1)
        tiles = lambda ap: ap.rearrange("(q p) d -> p q d", p=P)
        NLOADS = [0]

        @block.sync
        def _(sp):
            def load(dst, src):
                sp.dma_start(dst, src).then_inc(loads, 16)
                NLOADS[0] += 1

            load(w1[:, :], A["w1T"])
            load(tmp2[:, :], A["w2T"])
            load(columns[:, :], A["columns"])
            load(ln1g[:, :], col(A["L0_ffn_ln1_g"]))
            load(ln1b[:, :], col(A["L0_ffn_ln1_b"]))
            load(bias2[:, :], row(A["L0_ffn_b2"]).broadcast_to([P, D]))
            load(aw_z[:, :], A["L0_attn_W_in"][:, D:2 * D])
            load(ab_z[:, :], col(A["L0_attn_b_in"][D:2 * D]))
            load(aw_o[:, :], A["L0_attn_W_out"])
            load(ab_o[:, :], row(A["L0_attn_b_out"]).broadcast_to([P, D]))
            load(w_enc[:, :], A["L1_ffn_W_enc"])
            load(w_s2c[:, :, :], A["L1_ffn_W_s2c"].rearrange("(c p) m -> p c m", p=P))
            load(b_s2c[:, :], col(A["L1_ffn_b_s2c"]))
            load(w_r[0:MOE, :], A["L1_ffn_Wr"])
            load(w_r[MOE:MOE + 1, :], row(A["L1_ffn_br"]))
            load(w_e1[0:MOE, :, :], A["L1_ffn_W1"].rearrange("e m h -> m e h"))
            load(w_e1[MOE:MOE + 1, :, :], A["L1_ffn_b1"].rearrange("(a e) h -> a e h", a=1))
            load(w_e2[:, :, :], A["L1_ffn_W2"].rearrange("e h m -> h e m"))
            load(b_e2[:, :], A["moe_b2T"])
            load(w_c2s[0:MOE, :], A["L1_ffn_W_c2s"])
            load(w_dec[:, :, :], A["L1_ffn_W_dec"].rearrange("(c p) d -> p c d", p=P))
            load(b_dec[:, :], row(A["L1_ffn_b_dec"]).broadcast_to([P, D]))
            load(mlng[:, :], row(A["L1_ffn_ln_g"]).broadcast_to([P, D]))
            load(mlnb[:, :], row(A["L1_ffn_ln_b"]).broadcast_to([P, D]))
            load(mw_in[:, :], A["mamba_W_inT"])
            load(m_cw[:, :, :], A["L1_attn_conv_w"].rearrange("(c p) a k -> p c (a k)", p=P))
            load(mw_x[:, :, :], A["mamba_W_xT"].rearrange("(c p) m -> p c m", p=P))
            load(mw_dt[:, :], A["mamba_W_dtT"])
            load(mA[:, :, :], A["L1_attn_A_log"].rearrange("(c p) n -> p c n", p=P))
            load(mw_o[:, :, :], A["mamba_W_outT"].rearrange("(c p) d -> p c d", p=P))
            load(mb_o[:, :], row(A["L1_attn_b_out"]).broadcast_to([P, D]))
            sp.wait_ge(pool_const, 1)
            for k in range(3):
                at, of = 32 * k, 2 * D + STATES * k
                load(aw_s[:, at:at + STATES], A["L0_attn_W_in"][:, of:of + STATES])
                load(ab_s[at:at + STATES, :], col(A["L0_attn_b_in"][of:of + STATES]))
            load(aA[64:64 + STATES, :], col(A["L0_attn_A_log"]))
            assert NLOADS[0] == N_LOADS

            def load_x(i):
                if not first(i):
                    sp.wait_ge(FR.x_new.sem, FR.x_new.at(i - 1, 1))
                sp.dma_start(xin[:, :, :], tiles(A["L0_attn_x"][i, :, :])).then_inc(x_in.sem, 16)

            def store_x(i):
                sp.wait_ge(BK.x_new.sem, BK.x_new.at(i, 2))
                sp.dma_start(tiles(out[i, :, :]), xo[:, :, :]).then_inc(xo_free.sem, 16)

            load_x(0)
            load_x(1)
            with sp.Fori(2, BATCH) as i:
                load_x(i)
                store_x(i - 2)
            store_x(BATCH - 2)
            store_x(BATCH - 1)
            sp.wait_ge(xo_free.sem, xo_free.at(BATCH, 0))

        @block.gpsimd
        def _(pool):
            n = [0]

            def step(ins):
                ins.then_inc(iota_done, 1)
                n[0] += 1
                pool.wait_ge(iota_done, n[0])

            step(pool.memset(ab_s[:, :], 0.0))
            step(pool.memset(aA[:, :], 0.0))
            pool.memset(aw_s[:, :], 0.0).then_inc(pool_const, 1)
            pool.wait_ge(pool_const, 1)
            step(pool.memset(ones[:, :], 1.0))
            step(pool.memset(mean512[:, :], 1.0 / HIDDEN))
            step(pool.memset(neg_half[:, :], -0.5))
            step(pool.memset(xc[:, :, 0:TAPS - 1], 0.0))
            step(pool.memset(FR.cont[MOE:MOE + 1, :], 1.0))
            step(pool.memset(BK.cont[MOE:MOE + 1, :], 1.0))
            for k in range(2):
                starts = dA[:, k, :].rearrange("p (c t) -> p c t", t=CHUNK)[:, :, 0:1]
                step(pool.memset(starts, 0.0))
            step(pool.memset(ident[:, :], 0.0))
            step(pool.affine_select(out=ident[:, :], in_=ident[:, :], compare_op=ALU.not_equal, fill=1.0,
                                    base=0, pattern=[[-1, P]], channel_multiplier=1))
            step(pool.memset(earlier[:, :, :], 0.0))
            step(pool.affine_select(out=earlier[:, :, :], in_=earlier[:, :, :], compare_op=ALU.is_ge, fill=1.0,
                                    base=0, pattern=[[-1, EXPERTS], [1, EXPERTS]], channel_multiplier=0))
            step(pool.memset(sel[:, :, :], 0.0))
            for piece in range(3):
                step(pool.affine_select(out=sel[:, :, :], in_=sel[:, :, :], compare_op=ALU.not_equal, fill=1.0,
                                        base=-32 * piece, pattern=[[-1, 2 * STATES], [0, P]],
                                        channel_multiplier=1))
            pool.memset(w2[:, :, P:P + 2], 1.0 / HIDDEN).then_inc(pool_const, 1)
            pool.wait_ge(dve_setup, 2)

            def rstd(T, i, k, src, dst):
                pool.wait_ge(T.var.sem, T.var.at(i, k + 1))
                pool.tensor_tensor(out=dst, in0=src, in1=neg_half[:, :], op=ALU.pow).then_inc(T.rstd.sem, 1)

            def pre_add(T, i, l, x, bias, after):
                after()
                b = bias[:, :].rearrange("p (a d) -> p a d", a=1).broadcast_to([P, TILES, D])
                pool.tensor_tensor(out=T.xp[:, :, :], in0=x[:, :, :], in1=b,
                                   op=ALU.add).then_inc(T.xpre.sem, 1)

            def front(i):
                T = FR
                yield FFN
                pre_add(T, i, 0, xin, bias2, lambda: (pool.wait_ge(x_in.sem, x_in.at(i, 16)),
                                                      first(i) or pool.wait_ge(handed.sem, handed.at(i, 0))))
                rstd(T, i, 0, T.vv[:, :], T.rs[:, :])
                yield FFN + 4
                rstd(T, i, 1, fvar[:, :], frs[:, :])
                yield ATTN
                pre_add(T, i, 1, T.x, ab_o, lambda: pool.wait_ge(T.x_new.sem, T.x_new.at(i, 1)))
                rstd(T, i, 2, T.vv[:, :], T.rs[:, :])
                yield FFN_2
                pre_add(T, i, 2, T.x, bias2, lambda: pool.wait_ge(T.x_new.sem, T.x_new.at(i, 2)))
                rstd(T, i, 3, T.vv[:, :], T.rs[:, :])
                yield FFN_2 + 4
                rstd(T, i, 4, fvar[:, :], frs[:, :])
                yield MOE_F
                pre_add(T, i, 3, T.x, mlnb, lambda: pool.wait_ge(T.x_new.sem, T.x_new.at(i, 3)))
                rstd(T, i, 5, T.vv[:, :], T.rs[:, :])
                yield from moe(T, i, 6, MOE_F)

            def moe(T, i, k, s0):
                yield s0 + 12
                rstd(T, i, k, T.vv[:, :], T.rs[:, :])
                yield s0 + 13
                pool.wait_ge(T.ddn.sem, T.ddn.at(i, 1))
                g = mlng[:, :].rearrange("p (a d) -> p a d", a=1).broadcast_to([P, TILES, D])
                pool.tensor_tensor(out=T.dd[:, :, :], in0=T.dd[:, :, :], in1=g,
                                   op=ALU.mult).then_inc(T.ddg.sem, 1)

            def back(i):
                T = BK
                yield MAMBA
                pre_add(T, i, 0, hx, mb_o, lambda: (pool.wait_ge(handed.sem, handed.at(i, 1)),
                                                    pool.wait_ge(T.x_new.sem, T.x_new.at(i, 0))))
                rstd(T, i, 0, T.vv[:, :], T.rs[:, :])

                def drive(n_):
                    b = n_ % 2
                    pool.wait_ge(bbc_r.sem, bbc_r.at(i, n_ + 1))
                    if n_ >= 2:
                        pool.wait_ge(hs_r.sem, hs_r.at(i, n_ - 1))
                    in1 = bbc[:, b, :].rearrange("p (a t) -> p a t", a=1).broadcast_to([P, IC, SEQ])
                    pool.tensor_tensor(out=dbu[:, b, :].rearrange("p (c t) -> p c t", c=IC),
                                       in0=du[:, :, :], in1=in1, op=ALU.mult).then_inc(dbu_r.sem, 1)

                yield SCAN - 1
                pool.wait_ge(du_r.sem, du_r.at(i, 1))
                drive(0)
                for n_ in range(1, STATES):
                    yield SCAN + n_ - 1
                    drive(n_)
                yield MOE_B
                pre_add(T, i, 1, T.x, mlnb, lambda: pool.wait_ge(T.x_new.sem, T.x_new.at(i, 1)))
                rstd(T, i, 1, T.vv[:, :], T.rs[:, :])
                yield from moe(T, i, 2, MOE_B)

            alone(front(0))
            with pool.Fori(1, BATCH) as i:
                side_by_side(front(i), back(i - 1))
            alone(back(BATCH - 1))

        @block.vector
        def _(dve):
            n = [0]

            def step(ins):
                ins.then_inc(dve_f, 1)
                n[0] += 1
                dve.wait_ge(dve_f, n[0])

            dve.wait_ge(loads, 16 * N_LOADS)
            dve.wait_ge(pool_const, 2)
            w2v = tmp2[:, :]
            dve.wait_ge(pe_setup, 2)
            for k, w in enumerate((w1[:, :], w2v)):
                q = qs[:, 4 * k:4 * k + 4]
                step(dve.tensor_scalar(out=q[:, 0:1], in0=FR.ps[k][:, 0:1], scalar1=1.0 / (D * HIDDEN),
                                       scalar2=1e-5, op0=ALU.mult, op1=ALU.max))
                step(dve.reciprocal(out=q[:, 1:2], in_=q[:, 0:1]))
                step(dve.tensor_scalar(out=tmp[:, :], in0=w, scalar1=q[:, 1:2], scalar2=-0.5,
                                       op0=ALU.mult, op1=ALU.is_lt))
                step(dve.tensor_scalar(out=w, in0=w, scalar1=q[:, 1:2], scalar2=0.5,
                                       op0=ALU.mult, op1=ALU.is_gt))
                step(dve.tensor_tensor(out=w, in0=w, in1=tmp[:, :], op=ALU.subtract))
                dst = w1q[:, :] if k == 0 else w2q[:, :, :].rearrange("p c d -> p (c d)")
                step(dve.tensor_scalar(out=dst, in0=w, scalar1=q[:, 0:1], scalar2=None, op0=ALU.mult))
            step(dve.tensor_scalar(out=w1[:, :], in0=w1q[:, :], scalar1=ln1g[:, 0:1], scalar2=None, op0=ALU.mult))
            for c in range(HC):
                step(dve.tensor_scalar(out=w2[:, c, 0:P], in0=w2q[:, c, :], scalar1=ln2g[:, c:c + 1],
                                       scalar2=None, op0=ALU.mult))
                step(dve.tensor_scalar(out=tmp[:, c * P:(c + 1) * P], in0=w2q[:, c, :],
                                       scalar1=ln2b[:, c:c + 1], scalar2=None, op0=ALU.mult))
            for a in (b_enc[:, :], w_s2c[:, :, :], b_c2s[:, :], w_dec[:, :, :], mlng[:, :], mlnb[:, :],
                      mw_x[:, :, :]):
                step(dve.tensor_scalar(out=a, in0=a, scalar1=0.5, scalar2=None, op0=ALU.mult))
            step(dve.tensor_scalar(out=mw_o[:, :, :], in0=mw_o[:, :, :], scalar1=0.25, scalar2=None, op0=ALU.mult))
            dve.wait_ge(act_setup, 4)
            step(dve.tensor_scalar(out=mA[:, :, :], in0=mA[:, :, :], scalar1=-1.0, scalar2=None, op0=ALU.mult))
            step(dve.tensor_scalar(out=aA[:, :], in0=aA[:, :], scalar1=-1.0, scalar2=None, op0=ALU.mult))
            dve.memset(qs[:, 3:4], 0.0).then_inc(dve_setup, 1)
            dve.wait_ge(pe_setup, 3)
            for c in range(HC):
                step(dve.tensor_tensor(out=w2[:, c, 0:P], in0=w2[:, c, 0:P], in1=FR.po[0][:, 0:P],
                                       op=ALU.subtract))
            step(dve.tensor_tensor(out=bias2[:, :], in0=bias2[:, :], in1=FR.po[0][:, P:2 * P], op=ALU.add))
            step(dve.tensor_scalar(out=bias2[:, :], in0=bias2[:, :], scalar1=0.5, scalar2=None, op0=ALU.mult))
            step(dve.tensor_tensor(out=b1[:, :], in0=b1[:, :], in1=FR.po[0][:, 2 * P:2 * P + HC], op=ALU.add))
            step(dve.tensor_tensor(out=b_dec[:, :], in0=b_dec[:, :], in1=FR.po[1][:, 0:P], op=ALU.add))
            step(dve.tensor_tensor(out=b_s2c[:, :], in0=b_s2c[:, :], in1=FR.po[1][0:MOE, P:P + 1], op=ALU.add))
            step(dve.tensor_copy(out=w_c2s[MOE:MOE + EXPERTS, :], in_=FR.ps[1][0:EXPERTS, 0:ENC]))
            dve.memset(qs[:, 3:4], 0.0).then_inc(dve_setup, 1)
            SET = n[0]
            for sig in (FR.x_new, BK.x_new, xo_free):
                dve.sem_inc(sig.sem, sig.start)

            def norm(T, ch, i, l, k, x, double, step, sig=None):
                for q in range(TILES):
                    ch.add(dve.bn_stats(out=T.st[:, q, :], in_=x[:, q, :]))
                ch.wait()
                dve.memset(T.vv[:, 0:1], 0.0)
                for q in range(TILES):
                    ch.add(dve.bn_aggr(out=T.mv[:, q, :], in_=T.st[:, q, :]))
                ch.wait()
                s1, s2 = (1.0 + EPS, EPS * EPS) if double else (1.0, EPS)
                dve.tensor_scalar(out=T.vv[:, :], in0=T.mv[:, :, 1], scalar1=s1, scalar2=s2,
                                  op0=ALU.mult, op1=ALU.add).then_inc(T.var.sem, 1)
                yield step
                dve.wait_ge(T.rstd.sem, T.rstd.at(i, k + 1))
                for q in range(TILES):
                    ins = dve.tensor_scalar(out=(T.z if sig is None else T.dd)[:, q, :], in0=x[:, q, :],
                                            scalar1=T.mv[:, q, 0:1], scalar2=T.rs[:, q:q + 1],
                                            op0=ALU.subtract, op1=ALU.mult)
                    if sig is None:
                        ins.then_inc(T.zn.sem, 1)
                    elif q < TILES - 1:
                        ch.add(ins)
                    else:
                        ins.then_inc(sig.sem, 1)

            def ffn(ch, i, f, l, k, x, x_ready, s0):
                T = FR
                yield s0
                x_ready()
                yield from norm(T, ch, i, l, k, x, True, s0 + 1)
                for c in range(HC):
                    if c % 2 == 0:
                        yield s0 + 2 + c // 2
                    dve.wait_ge(h_r.sem, h_r.at(i, f * HC + c + 1))
                    dve.tensor_tensor(out=sq[:, c, :], in0=hT[:, c, :], in1=hT[:, c, :],
                                      op=ALU.mult).then_inc(sq_r.sem, 1)
                yield s0 + 4
                dve.wait_ge(fo_ps.sem, fo_ps.at(i, f + 1))
                for b in range(2):
                    stat = T.po[b][:, :].rearrange("p (q n) -> p q n", q=2)[:, :, P:P + 2]
                    ch.add(dve.tensor_copy(out=fs[:, b, :, :], in_=stat))
                ch.wait()
                mean = fs[:, :, :, 0]
                ch.add(dve.tensor_tensor(out=fvar[:, :].rearrange("p (b q) -> p b q", b=2), in0=mean, in1=mean,
                                         op=ALU.mult))
                ch.wait()
                ch.add(dve.scalar_tensor_tensor(out=fvar[:, :].rearrange("p (b q) -> p b q", b=2),
                                                in0=fs[:, :, :, 1], scalar=EPS,
                                                in1=fvar[:, :].rearrange("p (b q) -> p b q", b=2),
                                                op0=ALU.add, op1=ALU.subtract))
                ch.wait()
                dve.tensor_scalar(out=fvar[:, :], in0=fvar[:, :], scalar1=EPS, scalar2=None,
                                  op0=ALU.max).then_inc(T.var.sem, 1)
                yield s0 + 5
                dve.wait_ge(T.rstd.sem, T.rstd.at(i, k + 2))
                ch.add(dve.tensor_scalar(out=frs[:, :], in0=frs[:, :], scalar1=0.5, scalar2=None, op0=ALU.mult))
                ch.wait()
                dve.wait_ge(T.xpre.sem, T.xpre.at(i, l + 1))
                for q in range(TILES):
                    src = T.po[q // 2][:, (q % 2) * 256:(q % 2) * 256 + D]
                    ins = dve.scalar_tensor_tensor(out=T.x[:, q, :], in0=src, scalar=frs[:, q:q + 1],
                                                   in1=T.xp[:, q, :], op0=ALU.mult, op1=ALU.add)
                    if q < TILES - 1:
                        ch.add(ins)
                    else:
                        ins.then_inc(T.x_new.sem, 1)

            def attn(ch, i):
                T = FR
                yield ATTN
                dve.wait_ge(T.x_new.sem, T.x_new.at(i, 1))
                yield from norm(T, ch, i, 1, 2, T.x, False, ATTN + 1)
                yield ATTN + 2
                R = slice(64, 64 + STATES)
                dve.wait_ge(bcd_r.sem, bcd_r.at(i, 1))
                dve.wait_ge(aln_r.sem, aln_r.at(i, 1))
                dve.scalar_tensor_tensor(out=adt[R, 2, :], in0=bcd[R, :], scalar=0.0, in1=adt[R, 1, :],
                                         op0=ALU.max, op1=ALU.add).then_inc(adelta_r.sem, 1)
                yield ATTN + 3
                dve.wait_ge(adA_r.sem, adA_r.at(i, 1))
                ch.add(dve.tensor_tensor_scan(out=ah[32:32 + STATES, :], data0=adA[:, :], data1=bcd[0:STATES, :],
                                              initial=0.0, op0=ALU.mult, op1=ALU.add))
                ch.wait()
                dve.tensor_tensor(out=ap_[32:32 + STATES, :], in0=ah[32:32 + STATES, :],
                                  in1=bcd[32:32 + STATES, :], op=ALU.mult).then_inc(ap_r.sem, 1)
                yield ATTN + 4
                dve.wait_ge(ao_ps.sem, ao_ps.at(i, 1))
                ch.add(dve.tensor_copy(out=ay[:, :], in_=T.po[1][:, 0:TILES]))
                ch.wait()
                dve.wait_ge(T.xpre.sem, T.xpre.at(i, 2))
                for q in range(TILES):
                    ins = dve.scalar_tensor_tensor(out=T.x[:, q, :], in0=T.po[0][:, q * D:(q + 1) * D],
                                                   scalar=ay[:, q:q + 1], in1=T.xp[:, q, :],
                                                   op0=ALU.mult, op1=ALU.add)
                    if q < TILES - 1:
                        ch.add(ins)
                    else:
                        ins.then_inc(T.x_new.sem, 1)

            def moe(T, ch, i, l, k, dst, dst_sem, free, s0):
                yield s0
                dve.wait_ge(T.x_new.sem, T.x_new.at(i, l))
                yield from norm(T, ch, i, l, k, T.x, False, s0 + 1)
                yield s0 + 3
                dve.wait_ge(T.cont_ps.sem, T.cont_ps.at(i, 1))
                dve.tensor_scalar(out=T.cont[0:MOE, :], in0=T.ps[0][0:MOE, :], scalar1=b_s2c[:, :],
                                  scalar2=None, op0=ALU.add).then_inc(T.contr.sem, 1)
                yield s0 + 4
                dve.wait_ge(T.route_ps.sem, T.route_ps.at(i, 1))
                lgr = T.po[0][:, 0:TILES * EXPERTS].rearrange("p (q e) -> p q e", q=TILES)
                ch.add(dve.tensor_copy(out=T.lg[:, :, :], in_=lgr))
                ch.wait()
                ch.add(dve.reduce_max(out=T.mx[:, :], in_=T.lg[:, :, :], axis=AX))
                ch.wait()
                per_e = lambda a: a.rearrange("p (q a) -> p q a", a=1).broadcast_to([P, TILES, EXPERTS])
                dve.tensor_tensor(out=T.lg[:, :, :], in0=T.lg[:, :, :], in1=per_e(T.mx[:, :]),
                                  op=ALU.subtract).then_inc(T.lgr.sem, 1)
                dve.wait_ge(T.lgr.sem, T.lgr.at(i, 1))
                full = [P, TILES, EXPERTS, EXPERTS]
                lj = T.lg[:, :, :].rearrange("p q (a j) -> p q a j", a=1).broadcast_to(full)
                le = T.lg[:, :, :].rearrange("p q (e a) -> p q e a", a=1).broadcast_to(full)
                ch.add(dve.tensor_tensor(out=T.cmp[:, :, :, :], in0=lj, in1=le, op=ALU.is_gt))
                ch.add(dve.tensor_tensor(out=T.eq[:, :, :, :], in0=lj, in1=le, op=ALU.is_equal))
                ch.wait()
                low = earlier[:, :, :].rearrange("p (a e) j -> p a (e j)", a=1)\
                    .broadcast_to([P, TILES, EXPERTS * EXPERTS])
                eqf = T.eq[:, :, :, :].rearrange("p q e j -> p q (e j)")
                ch.add(dve.tensor_tensor(out=eqf, in0=eqf, in1=low, op=ALU.mult))
                ch.wait()
                ch.add(dve.tensor_tensor(out=T.cmp[:, :, :, :], in0=T.cmp[:, :, :, :], in1=T.eq[:, :, :, :],
                                         op=ALU.add))
                ch.wait()
                ch.add(dve.reduce_sum(out=T.rk[:, :, :], in_=T.cmp[:, :, :, :], axis=AX))
                ch.wait()
                yield s0 + 5
                dve.wait_ge(T.exr.sem, T.exr.at(i, 1))
                ch.add(dve.scalar_tensor_tensor(out=T.rk[:, :, :], in0=T.rk[:, :, :], scalar=1.5,
                                                in1=T.ex[:, :, :], op0=ALU.is_lt, op1=ALU.mult))
                ch.wait()
                ch.add(dve.reduce_sum(out=T.sm[:, :], in_=T.rk[:, :, :], axis=AX))
                ch.wait()
                ch.add(dve.reciprocal(out=T.sm[:, :], in_=T.sm[:, :]))
                ch.wait()
                ch.add(dve.tensor_tensor(out=T.eo[:, :, MOE:MOE + EXPERTS], in0=T.rk[:, :, :],
                                         in1=per_e(T.sm[:, :]), op=ALU.mult))
                ch.wait()
                for q in range(TILES):
                    if q % 2 == 0:
                        yield s0 + 8 + q // 2
                    dve.wait_ge(T.ye_ps.sem, T.ye_ps.at(i, q + 1))
                    y = T.po[q % 2][:, :].rearrange("p (e m) -> p e m", e=EXPERTS)
                    g = T.eo[:, q, MOE:MOE + EXPERTS].rearrange("p (e a) -> p e a", a=1)\
                        .broadcast_to([P, EXPERTS, MOE])
                    dve.tensor_tensor(out=T.gy[:, :, :], in0=y, in1=g, op=ALU.mult).then_inc(T.yer.sem, 1)
                    dve.wait_ge(T.yer.sem, T.yer.at(i, q + 1))
                    ins = dve.reduce_sum(out=T.eo[:, q, 0:MOE], in_=T.gy[:, :, :].rearrange("p e m -> p m e"),
                                         axis=AX)
                    if q < TILES - 1:
                        ch.add(ins)
                        ch.wait()
                    else:
                        ins.then_inc(T.eor.sem, 1)
                yield s0 + 12
                dve.wait_ge(T.dec_ps.sem, T.dec_ps.at(i, 1))
                bd = b_dec[:, :].rearrange("p (a d) -> p a d", a=1).broadcast_to([P, TILES, D])
                ch.add(dve.tensor_tensor(out=T.dd[:, :, :], in0=T.po[0][:, :].rearrange("p (q d) -> p q d", q=TILES),
                                         in1=bd, op=ALU.add))
                ch.wait()
                yield from norm(T, ch, i, None, k + 1, T.dd, False, s0 + 13, T.ddn)
                yield s0 + 14
                dve.wait_ge(T.ddg.sem, T.ddg.at(i, 1))
                dve.wait_ge(T.xpre.sem, T.xpre.at(i, l + 1))
                free()
                dve.tensor_tensor(out=dst[:, :, :], in0=T.xp[:, :, :], in1=T.dd[:, :, :],
                                  op=ALU.add).then_inc(dst_sem.sem, 1)

            def front(i):
                ch = Chain(dve, dve_f, DVE_F, i)
                ch.n = SET
                T = FR

                yield from ffn(ch, i, 0, 0, 0, xin, lambda: dve.wait_ge(x_in.sem, x_in.at(i, 16)), FFN)
                yield from attn(ch, i)
                yield from ffn(ch, i, 1, 2, 3, T.x, lambda: dve.wait_ge(T.x_new.sem, T.x_new.at(i, 2)), FFN_2)

                def free():
                    if not first(i):
                        dve.wait_ge(BK.x_new.sem, BK.x_new.at(i - 1, 1))

                yield from moe(T, ch, i, 3, 5, hx, handed, free, MOE_F)
                assert ch.n - SET == DVE_F, ch.n - SET

            def back(i):
                ch = Chain(dve, dve_b, DVE_B, i)
                T = BK
                yield MAMBA
                dve.wait_ge(handed.sem, handed.at(i, 1))
                yield from norm(T, ch, i, 0, 0, hx, False, MAMBA + 1)
                yield MAMBA + 3
                dve.wait_ge(min_r.sem, min_r.at(i, IC))
                for c in range(IC):
                    ch.add(dve.tensor_scalar(out=cv[:, 0, c, :], in0=xc[:, c, 0:SEQ], scalar1=m_cw[:, c, 0:1],
                                             scalar2=m_cb[:, c:c + 1], op0=ALU.mult, op1=ALU.add))
                ch.wait()
                for c in range(IC):
                    ch.add(dve.scalar_tensor_tensor(out=cv[:, 1, c, :], in0=xc[:, c, 1:1 + SEQ],
                                                    scalar=m_cw[:, c, 1:2], in1=cv[:, 0, c, :],
                                                    op0=ALU.mult, op1=ALU.add))
                ch.wait()
                for c in range(IC):
                    ins = dve.scalar_tensor_tensor(out=cv[:, 0, c, :], in0=xc[:, c, 2:2 + SEQ],
                                                   scalar=m_cw[:, c, 2:3], in1=cv[:, 1, c, :],
                                                   op0=ALU.mult, op1=ALU.add)
                    if c < IC - 1:
                        ch.add(ins)
                    else:
                        ins.then_inc(cv_r.sem, 1)
                yield MAMBA + 4
                dve.wait_ge(cth_r.sem, cth_r.at(i, 1))
                dve.scalar_tensor_tensor(out=u2[:, :, :], in0=cth[:, :, :], scalar=1.0, in1=cv[:, 0, :, :],
                                         op0=ALU.add, op1=ALU.mult).then_inc(u2_r.sem, 1)
                dve.wait_ge(rth_r.sem, rth_r.at(i, 1))
                ch.add(dve.scalar_tensor_tensor(out=g4[:, :, :], in0=rth[:, :, :], scalar=1.0, in1=res[:, :, :],
                                                op0=ALU.add, op1=ALU.mult))
                yield MAMBA + 5
                dve.wait_ge(bcf_r.sem, bcf_r.at(i, 1))
                R = slice(64, 96)
                ch.add(dve.tensor_copy(out=bch[R, 0, :], in_=bc[R, 0, :]))
                ch.wait()
                ch.add(dve.tensor_tensor(out=bc[R, 1, :], in0=bc[R, 0, :], in1=bch[R, 0, :], op=ALU.subtract))
                dve.tensor_copy(out=bc3[0:32, :], in_=bch[R, 0, :]).then_inc(bc3_r.sem, 1)
                ch.wait()
                ch.add(dve.tensor_copy(out=bch[R, 1, :], in_=bc[R, 1, :]))
                ch.wait()
                dve.tensor_tensor(out=bc3[R, :], in0=bc[R, 1, :], in1=bch[R, 1, :],
                                  op=ALU.subtract).then_inc(bc3_r.sem, 1)
                dve.tensor_copy(out=bc3[32:64, :], in_=bch[R, 1, :]).then_inc(bc3_r.sem, 1)
                yield MAMBA + 6
                for c in range(IC):
                    dve.wait_ge(mabs_r.sem, mabs_r.at(i, c + 1))
                    dve.tensor_scalar(out=delta[:, c, :], in0=T.ps[c][:, :], scalar1=mb_dt[:, c:c + 1],
                                      scalar2=0.0, op0=ALU.add, op1=ALU.max).then_inc(mrelu_r.sem, 1)
                dve.wait_ge(mln_r.sem, mln_r.at(i, 1))
                dve.wait_ge(mrelu_r.sem, mrelu_r.at(i, IC))
                dve.tensor_tensor(out=delta[:, :, :], in0=delta[:, :, :], in1=dex[:, :, :],
                                  op=ALU.add).then_inc(delta_r.sem, 1)
                dve.wait_ge(delta_r.sem, delta_r.at(i, 1))
                dve.tensor_tensor(out=du[:, :, :], in0=delta[:, :, :], in1=u2[:, :, :],
                                  op=ALU.mult).then_inc(du_r.sem, 1)

                def read_out(n_):
                    b = n_ % 2
                    dve.wait_ge(cbc_ps.sem, cbc_ps.at(i, n_ + 1))
                    dve.wait_ge(hs_r.sem, hs_r.at(i, n_ + 1))
                    if n_ >= 2:
                        dve.wait_ge(sum_ps.sem, sum_ps.at(i, n_ - 1))
                    c_n = T.ps[1][:, :].rearrange("p (a t) -> p a t", a=1).broadcast_to([P, IC, SEQ])
                    v = lambda a: a.rearrange("p (c t) -> p c t", c=IC)
                    dve.tensor_tensor(out=v(hc[:, b, :]), in0=v(hs[:, b, :]), in1=c_n,
                                      op=ALU.mult).then_inc(hc_r.sem, 1)

                for n_ in range(STATES):
                    yield SCAN + n_
                    b = n_ % 2
                    dve.wait_ge(dA_r.sem, dA_r.at(i, n_ + 1))
                    dve.wait_ge(dbu_r.sem, dbu_r.at(i, n_ + 1))
                    if n_ >= 2:
                        dve.wait_ge(hc_r.sem, hc_r.at(i, n_ - 1))
                    dve.tensor_tensor_scan(out=hs[:, b, :], data0=dA[:, b, :], data1=dbu[:, b, :],
                                           initial=0.0, op0=ALU.mult, op1=ALU.add).then_inc(hs_r.sem, 1)
                    read_out(n_)
                yield MAMBA_OUT
                dve.wait_ge(sum_ps.sem, sum_ps.at(i, STATES))
                for c in range(IC):
                    ins = dve.tensor_tensor(out=yg[:, c, :], in0=T.po[c][:, :], in1=g4[:, c, :], op=ALU.mult)
                    if c < IC - 1:
                        ch.add(ins)
                    else:
                        ins.then_inc(yg_r.sem, 1)
                yield MAMBA_OUT + 1
                dve.wait_ge(mo_ps.sem, mo_ps.at(i, 1))
                dve.wait_ge(T.xpre.sem, T.xpre.at(i, 1))
                dve.tensor_tensor(out=T.x[:, :, :], in0=T.ps[0][:, :].rearrange("p (q d) -> p q d", q=TILES),
                                  in1=T.xp[:, :, :], op=ALU.add).then_inc(T.x_new.sem, 1)

                def free():
                    dve.wait_ge(xo_free.sem, xo_free.at(i, 0))

                yield from moe(T, ch, i, 1, 1, xo, T.x_new, free, MOE_B)
                assert ch.n == DVE_B, ch.n

            alone(front(0))
            with dve.Fori(1, BATCH) as i:
                side_by_side(front(i), back(i - 1))
            alone(back(BATCH - 1))

        @block.scalar
        def _(act):
            loaded = [None]

            def table(func):
                sets = {ACT.Gelu: ["gelu_and_others"], ACT.Tanh: ["exp_and_others", "gelu_and_others"],
                        ACT.Exp: ["exp_and_others", "natural_log_exp_and_others"],
                        ACT.Ln: ["natural_log_exp_and_others"]}[func]
                if loaded[0] not in sets:
                    act.preload_act_table_set(sets[0])
                    loaded[0] = sets[0]

            act.wait_ge(loads, 16 * N_LOADS)
            act.activation(out=tmp[:, :], in_=w1[:, :], func=ACT.Abs, accum_out=qs[:, 2:3]).then_inc(act_setup, 1)
            act.wait_ge(act_setup, 1)
            act.activation(out=tmp[:, :], in_=tmp2[:, :], func=ACT.Abs, accum_out=qs[:, 6:7]).then_inc(act_setup, 1)
            table(ACT.Exp)
            act.activation(out=mA[:, :, :], in_=mA[:, :, :], func=ACT.Exp).then_inc(act_setup, 1)
            act.activation(out=aA[:, :], in_=aA[:, :], func=ACT.Exp).then_inc(act_setup, 1)
            act.wait_ge(dve_setup, 2)

            def zt(T, i, l):
                act.wait_ge(T.zt_ps.sem, T.zt_ps.at(i, l + 1))
                act.activation(out=T.zT[:, :], in_=T.ps[0][:, :], func=ACT.Copy).then_inc(T.zt.sem, 1)

            def ffn(i, f, l, s0):
                yield s0 + 1
                zt(FR, i, l)
                for c in range(HC):
                    if c % 2 == 0:
                        yield s0 + 2 + c // 2
                        table(ACT.Gelu)
                    act.wait_ge(h_ps.sem, h_ps.at(i, f * HC + c + 1))
                    act.activation(out=hT[:, c, :], in_=FR.ps[(c + 1) % 2][:, :], func=ACT.Gelu,
                                   bias=b1[:, c:c + 1]).then_inc(h_r.sem, 1)

            def attn(i):
                T = FR
                R = slice(64, 64 + STATES)
                yield ATTN + 1
                zt(T, i, 1)
                yield ATTN + 2
                table(ACT.Gelu)
                act.wait_ge(az_ps.sem, az_ps.at(i, 1))
                act.activation(out=gz[:, :], in_=T.ps[1][:, :], func=ACT.Gelu, bias=ab_z[:, :]).then_inc(gz_r.sem, 1)
                table(ACT.Ln)
                act.wait_ge(as_ps.sem, as_ps.at(i, 1))
                act.activation(out=bcd[:, :], in_=T.ps[0][0:96, :], func=ACT.Identity,
                               bias=ab_s[:, :]).then_inc(bcd_r.sem, 1)
                ch = Chain(act, act_f, ACT_F, i)
                act.wait_ge(bcd_r.sem, bcd_r.at(i, 1))
                ch.add(act.activation(out=adt[R, 0, :], in_=bcd[R, :], func=ACT.Abs))
                ch.wait()
                ch.add(act.activation(out=adt[R, 0, :], in_=adt[R, 0, :], func=ACT.Exp, scale=-1.0))
                ch.wait()
                act.activation(out=adt[R, 1, :], in_=adt[R, 0, :], func=ACT.Ln, bias=1.0).then_inc(aln_r.sem, 1)
                yield ATTN + 3
                table(ACT.Exp)
                act.wait_ge(adelta_r.sem, adelta_r.at(i, 1))
                act.activation(out=adA[:, :], in_=adt[R, 2, :], func=ACT.Exp,
                               scale=aA[R, :]).then_inc(adA_r.sem, 1)
                assert ch.n == ACT_F

            def moe(T, i, l, s0):
                yield s0 + 1
                zt(T, i, l)
                yield s0 + 2
                table(ACT.Tanh)
                for c in range(EC):
                    act.wait_ge(T.enc_ps.sem, T.enc_ps.at(i, c + 1))
                    act.activation(out=T.s1[:, c, :], in_=T.ps[(c + 1) % 2][:, :], func=ACT.Tanh,
                                   bias=b_enc[:, c:c + 1], scale=0.5).then_inc(T.s1r.sem, 1)
                for e in range(EXPERTS):
                    if e % 2 == 0:
                        yield s0 + 4 + e // 2
                    act.wait_ge(T.he_ps.sem, T.he_ps.at(i, e + 1))
                    act.activation(out=T.he[:, e, :], in_=T.ps[(e + 1) % 2][:, :],
                                   func=ACT.Relu).then_inc(T.her.sem, 1)
                    if e == 1:
                        table(ACT.Exp)
                        act.wait_ge(T.lgr.sem, T.lgr.at(i, 1))
                        act.activation(out=T.ex[:, :, :], in_=T.lg[:, :, :], func=ACT.Exp).then_inc(T.exr.sem, 1)
                yield s0 + 10
                act.wait_ge(T.eoT_ps.sem, T.eoT_ps.at(i, 1))
                act.activation(out=T.eoT[:, :], in_=T.ps[0][0:MOE + EXPERTS, :],
                               func=ACT.Copy).then_inc(T.eoTr.sem, 1)
                yield s0 + 11
                table(ACT.Tanh)
                for c in range(EC):
                    act.wait_ge(T.c2s_ps.sem, T.c2s_ps.at(i, c + 1))
                    act.activation(out=T.s1[:, c, :], in_=T.ps[(c + 1) % 2][:, :], func=ACT.Tanh,
                                   bias=b_c2s[:, c:c + 1], scale=0.5).then_inc(T.s2r.sem, 1)

            def front(i):
                yield from ffn(i, 0, 0, FFN)
                yield from attn(i)
                yield from ffn(i, 1, 2, FFN_2)
                yield from moe(FR, i, 3, MOE_F)

            def back(i):
                T = BK
                yield MAMBA + 1
                zt(T, i, 0)
                for c in range(2 * IC):
                    if c % 2 == 0:
                        yield MAMBA + 2 + c // 2
                    act.wait_ge(min_ps.sem, min_ps.at(i, c + 1))
                    dst = xc[:, c, TAPS - 1:] if c < IC else res[:, c - IC, :]
                    act.activation(out=dst, in_=T.ps[(c + 1) % 2][:, :], func=ACT.Identity,
                                   bias=mb_in[:, c:c + 1]).then_inc(min_r.sem, 1)
                yield MAMBA + 4
                table(ACT.Tanh)
                act.wait_ge(cv_r.sem, cv_r.at(i, 1))
                act.activation(out=cth[:, :, :], in_=cv[:, 0, :, :], func=ACT.Tanh, scale=0.5).then_inc(cth_r.sem, 1)
                act.wait_ge(min_r.sem, min_r.at(i, 2 * IC))
                act.activation(out=rth[:, :, :], in_=res[:, :, :], func=ACT.Tanh, scale=0.5).then_inc(rth_r.sem, 1)
                yield MAMBA + 5
                act.wait_ge(mx_ps.sem, mx_ps.at(i, 1))
                act.activation(out=dlt[:, :], in_=T.ps[1][0:RANK, :], func=ACT.Copy).then_inc(dlt_r.sem, 1)
                act.activation(out=bc[64:96, 0, :], in_=T.ps[1][64:96, :], func=ACT.Copy).then_inc(bcf_r.sem, 1)
                yield MAMBA + 6
                table(ACT.Ln)
                for c in range(IC):
                    act.wait_ge(mdt_ps.sem, mdt_ps.at(i, c + 1))
                    act.activation(out=dab[:, c, :], in_=T.ps[c][:, :], func=ACT.Abs,
                                   bias=mb_dt[:, c:c + 1]).then_inc(mabs_r.sem, 1)
                ch = Chain(act, act_b, ACT_B, i)
                act.wait_ge(mabs_r.sem, mabs_r.at(i, IC))
                ch.add(act.activation(out=dab[:, :, :], in_=dab[:, :, :], func=ACT.Exp, scale=-1.0))
                ch.wait()
                act.activation(out=dex[:, :, :], in_=dab[:, :, :], func=ACT.Ln, bias=1.0).then_inc(mln_r.sem, 1)
                act.wait_ge(delta_r.sem, delta_r.at(i, 1))

                def decay(n_):
                    b = n_ % 2
                    act.wait_ge(bbc_ps.sem, bbc_ps.at(i, n_ + 1))
                    if n_ >= 2:
                        act.wait_ge(dbu_r.sem, dbu_r.at(i, n_ - 1))
                    act.activation(out=bbc[:, b, :], in_=T.ps[0][:, :], func=ACT.Copy).then_inc(bbc_r.sem, 1)
                    if n_ >= 2:
                        act.wait_ge(hs_r.sem, hs_r.at(i, n_ - 1))
                    for c in range(IC):
                        dst = dA[:, b, c * SEQ:(c + 1) * SEQ].rearrange("p (k t) -> p k t", t=CHUNK)[:, :, 1:]
                        src = delta[:, c, :].rearrange("p (k t) -> p k t", t=CHUNK)[:, :, 1:]
                        ins = act.activation(out=dst, in_=src, func=ACT.Exp, scale=mA[:, c, n_:n_ + 1])
                        if c < IC - 1:
                            ch.add(ins)
                        else:
                            ins.then_inc(dA_r.sem, 1)

                decay(0)
                for n_ in range(1, STATES):
                    yield SCAN + n_ - 1
                    table(ACT.Exp)
                    decay(n_)
                assert ch.n == ACT_B, ch.n
                yield from moe(T, i, 1, MOE_B)

            alone(front(0))
            with act.Fori(1, BATCH) as i:
                loaded[0] = None
                side_by_side(front(i), back(i - 1))
            alone(back(BATCH - 1))

        @block.tensor
        def _(pe):
            pe.wait_ge(pool_const, 2)
            for k in range(2):
                pe.wait_ge(act_setup, k + 1)
                pe.matmul(FR.ps[k][:, 0:1], lhsT=ones[:, :], rhs=qs[:, 4 * k + 2:4 * k + 3],
                          start=True, stop=True).then_inc(pe_setup, 1)
            pe.wait_ge(dve_setup, 1)

            def total(dst, lhs, rhs, m):
                for c in range(m):
                    last = pe.matmul(dst, lhsT=lhs(c), rhs=rhs(c), start=(c == 0), stop=(c == m - 1))
                return last
            total(FR.po[0][:, 0:P], lambda c: mean512[:, :], lambda c: w2[:, c, 0:P], HC)
            total(FR.po[0][:, P:2 * P], lambda c: ones[:, :], lambda c: tmp[:, c * P:(c + 1) * P], HC)
            for j in range(HC):
                pe.matmul(FR.po[0][:, 2 * P + j:2 * P + j + 1], lhsT=w1q[:, j * P:(j + 1) * P], rhs=ln1b[:, :],
                          start=True, stop=True)
            total(FR.po[1][:, 0:P], lambda c: ones[:, :], lambda c: w_dec[:, c, :], EC)
            total(FR.po[1][0:MOE, P:P + 1], lambda c: w_s2c[:, c, :], lambda c: ones[:, 0:1], EC)
            pe.matmul(FR.ps[1][0:EXPERTS, 0:ENC], lhsT=b_e2[:, :], rhs=w_c2s[0:MOE, :],
                      start=True, stop=True).then_inc(pe_setup, 1)
            pe.wait_ge(dve_setup, 2)

            def zt(T, i, l):
                for q in range(TILES):
                    pe.wait_ge(T.zn.sem, T.zn.at(i, l * TILES + q + 1))
                    last = pe.transpose(T.ps[0][:, q * P:(q + 1) * P], in_=T.z[:, q, :], identity=ident[:, :])
                last.then_inc(T.zt_ps.sem, 1)

            def ffn(i, f, l, s0):
                T = FR
                yield s0 + 1
                zt(T, i, l)
                yield s0 + 2
                pe.wait_ge(T.zt.sem, T.zt.at(i, l + 1))
                for c in range(HC):
                    if c == 2:
                        yield s0 + 3
                    if c >= 2:
                        pe.wait_ge(h_r.sem, h_r.at(i, f * HC + c - 1))
                    pe.matmul(T.ps[(c + 1) % 2][:, :], lhsT=w1[:, c * P:(c + 1) * P], rhs=T.zT[:, :],
                              start=True, stop=True).then_inc(h_ps.sem, 1)
                yield s0 + 4
                pe.wait_ge(h_r.sem, h_r.at(i, f * HC + HC))
                pe.wait_ge(sq_r.sem, sq_r.at(i, f * HC + HC))
                for q in range(TILES):
                    o = T.po[q // 2][:, (q % 2) * 256:(q % 2) * 256 + P + 2]
                    for c in range(HC):
                        pe.matmul(o[:, 0:P + 1], lhsT=hT[:, c, q * P:(q + 1) * P], rhs=w2[:, c, 0:P + 1],
                                  start=(c == 0), stop=(c == HC - 1))
                    for c in range(HC):
                        last = pe.matmul(o[:, P + 1:P + 2], lhsT=sq[:, c, q * P:(q + 1) * P],
                                         rhs=w2[:, c, P + 1:P + 2], start=(c == 0), stop=(c == HC - 1))
                last.then_inc(fo_ps.sem, 1)

            def attn(i):
                T = FR
                yield ATTN + 1
                zt(T, i, 1)
                yield ATTN + 2
                pe.wait_ge(T.zt.sem, T.zt.at(i, 2))
                pe.matmul(T.ps[1][:, :], lhsT=aw_z[:, :], rhs=T.zT[:, :], start=True, stop=True).then_inc(az_ps.sem, 1)
                pe.matmul(T.ps[0][0:96, :], lhsT=aw_s[:, :], rhs=T.zT[:, :], start=True,
                          stop=True).then_inc(as_ps.sem, 1)
                yield ATTN + 3
                pe.wait_ge(gz_r.sem, gz_r.at(i, 1))
                for q in range(TILES):
                    pe.matmul(T.po[0][:, q * P:(q + 1) * P], lhsT=gz[:, q * P:(q + 1) * P], rhs=aw_o[:, :],
                              start=True, stop=True)
                pe.wait_ge(ap_r.sem, ap_r.at(i, 1))
                for q in range(TILES):
                    last = pe.matmul(T.po[1][:, q:q + 1], lhsT=ap_[32:32 + STATES, q * P:(q + 1) * P],
                                     rhs=ones[32:32 + STATES, 0:1], start=True, stop=True)
                last.then_inc(ao_ps.sem, 1)

            def moe(T, i, l, s0):
                yield s0 + 1
                zt(T, i, l)
                yield s0 + 2
                pe.wait_ge(T.zt.sem, T.zt.at(i, l + 1))
                for c in range(EC):
                    pe.matmul(T.ps[(c + 1) % 2][:, :], lhsT=w_enc[:, c * P:(c + 1) * P], rhs=T.zT[:, :],
                              start=True, stop=True).then_inc(T.enc_ps.sem, 1)
                yield s0 + 3
                pe.wait_ge(T.s1r.sem, T.s1r.at(i, EC))
                for c in range(EC):
                    last = pe.matmul(T.ps[0][0:MOE, :], lhsT=w_s2c[:, c, :], rhs=T.s1[:, c, :],
                                     start=(c == 0), stop=(c == EC - 1))
                last.then_inc(T.cont_ps.sem, 1)
                yield s0 + 4
                pe.wait_ge(T.contr.sem, T.contr.at(i, 1))
                for q in range(TILES):
                    last = pe.matmul(T.po[0][:, q * EXPERTS:(q + 1) * EXPERTS],
                                     lhsT=T.cont[:, q * P:(q + 1) * P], rhs=w_r[:, :], start=True, stop=True)
                last.then_inc(T.route_ps.sem, 1)
                for e in range(EXPERTS):
                    if e >= 2 and e % 2 == 0:
                        yield s0 + 4 + e // 2
                    if e >= 2:
                        pe.wait_ge(T.her.sem, T.her.at(i, e - 1))
                    pe.matmul(T.ps[(e + 1) % 2][:, :], lhsT=w_e1[:, e, :], rhs=T.cont[:, :],
                              start=True, stop=True).then_inc(T.he_ps.sem, 1)
                yield s0 + 8
                pe.wait_ge(T.her.sem, T.her.at(i, EXPERTS))
                pe.wait_ge(T.lgr.sem, T.lgr.at(i, 1))
                for q in range(TILES):
                    if q == 2:
                        yield s0 + 9
                    if q >= 2:
                        pe.wait_ge(T.yer.sem, T.yer.at(i, q - 1))
                    for e in range(EXPERTS):
                        last = pe.matmul(T.po[q % 2][:, e * MOE:(e + 1) * MOE],
                                         lhsT=T.he[:, e, q * P:(q + 1) * P], rhs=w_e2[:, e, :],
                                         start=True, stop=True)
                    last.then_inc(T.ye_ps.sem, 1)
                yield s0 + 10
                pe.wait_ge(T.eor.sem, T.eor.at(i, 1))
                for q in range(TILES):
                    last = pe.transpose(T.ps[0][0:MOE + EXPERTS, q * P:(q + 1) * P], in_=T.eo[:, q, :],
                                        identity=ident[:, :])
                last.then_inc(T.eoT_ps.sem, 1)
                yield s0 + 11
                pe.wait_ge(T.eoTr.sem, T.eoTr.at(i, 1))
                for c in range(EC):
                    pe.matmul(T.ps[(c + 1) % 2][:, :], lhsT=w_c2s[:, c * P:(c + 1) * P], rhs=T.eoT[:, :],
                              start=True, stop=True).then_inc(T.c2s_ps.sem, 1)
                yield s0 + 12
                pe.wait_ge(T.s2r.sem, T.s2r.at(i, EC))
                for q in range(TILES):
                    for c in range(EC):
                        last = pe.matmul(T.po[0][:, q * P:(q + 1) * P], lhsT=T.s1[:, c, q * P:(q + 1) * P],
                                         rhs=w_dec[:, c, :], start=(c == 0), stop=(c == EC - 1))
                last.then_inc(T.dec_ps.sem, 1)

            def front(i):
                yield from ffn(i, 0, 0, FFN)
                yield from attn(i)
                yield from ffn(i, 1, 2, FFN_2)
                yield from moe(FR, i, 3, MOE_F)

            def back(i):
                T = BK
                yield MAMBA + 1
                zt(T, i, 0)
                yield MAMBA + 2
                pe.wait_ge(T.zt.sem, T.zt.at(i, 1))
                for c in range(2 * IC):
                    if c == 2:
                        yield MAMBA + 3
                    if c >= 2:
                        pe.wait_ge(min_r.sem, min_r.at(i, c - 1))
                    pe.matmul(T.ps[(c + 1) % 2][:, :], lhsT=mw_in[:, c * P:(c + 1) * P], rhs=T.zT[:, :],
                              start=True, stop=True).then_inc(min_ps.sem, 1)
                yield MAMBA + 5
                pe.wait_ge(min_r.sem, min_r.at(i, 2 * IC))
                pe.wait_ge(u2_r.sem, u2_r.at(i, 1))
                for c in range(IC):
                    last = pe.matmul(T.ps[1][0:96, :], lhsT=mw_x[:, c, :], rhs=u2[:, c, :],
                                     start=(c == 0), stop=(c == IC - 1))
                last.then_inc(mx_ps.sem, 1)
                yield MAMBA + 6
                pe.wait_ge(dlt_r.sem, dlt_r.at(i, 1))
                pe.wait_ge(bcf_r.sem, bcf_r.at(i, 1))
                for c in range(IC):
                    pe.matmul(T.ps[c][:, :], lhsT=mw_dt[:, c * P:(c + 1) * P], rhs=dlt[:, :],
                              start=True, stop=True).then_inc(mdt_ps.sem, 1)
                pe.wait_ge(bc3_r.sem, bc3_r.at(i, 3))
                pe.wait_ge(mrelu_r.sem, mrelu_r.at(i, IC))

                def add_up(n_):
                    pe.wait_ge(hc_r.sem, hc_r.at(i, n_ + 1))
                    for c in range(IC):
                        last = pe.matmul(T.po[c][:, :], lhsT=ident[:, :], rhs=hc[:, n_ % 2, c * SEQ:(c + 1) * SEQ],
                                         start=(n_ == 0), stop=(n_ == STATES - 1))
                    last.then_inc(sum_ps.sem, 1)

                def spread_b(n_):
                    if n_ >= 1:
                        pe.wait_ge(bbc_r.sem, bbc_r.at(i, n_))
                    pe.matmul(T.ps[0][:, :], lhsT=sel[:, n_, :], rhs=bc3[:, :], start=True,
                              stop=True).then_inc(bbc_ps.sem, 1)

                spread_b(0)
                for n_ in range(STATES):
                    yield SCAN + n_
                    if n_ < STATES - 1:
                        spread_b(n_ + 1)
                    if n_ >= 1:
                        pe.wait_ge(hc_r.sem, hc_r.at(i, n_))
                    pe.matmul(T.ps[1][:, :], lhsT=sel[:, STATES + n_, :], rhs=bc3[:, :], start=True,
                              stop=True).then_inc(cbc_ps.sem, 1)
                    if n_ >= 1:
                        add_up(n_ - 1)
                yield SCAN + STATES
                add_up(STATES - 1)
                yield MAMBA_OUT
                pe.wait_ge(yg_r.sem, yg_r.at(i, 1))
                for q in range(TILES):
                    for c in range(IC):
                        last = pe.matmul(T.ps[0][:, q * P:(q + 1) * P], lhsT=yg[:, c, q * P:(q + 1) * P],
                                         rhs=mw_o[:, c, :], start=(c == 0), stop=(c == IC - 1))
                last.then_inc(mo_ps.sem, 1)
                yield MOE_B + 1
                pe.wait_ge(T.x_new.sem, T.x_new.at(i, 1))
                yield from moe(T, i, 1, MOE_B)

            alone(front(0))
            with pe.Fori(1, BATCH) as i:
                side_by_side(front(i), back(i - 1))
            alone(back(BATCH - 1))


N_LOADS = 31 + 7
COLUMNS = {"L0_ffn_ln2_g": HC, "L0_ffn_ln2_b": HC, "L0_ffn_b1": HC, "L1_ffn_b_enc": EC, "L1_ffn_b_c2s": EC,
           "L1_attn_b_in": 2 * IC, "L1_attn_conv_b": IC, "L1_attn_b_dt": IC}
COLUMNS_AT = [sum(list(COLUMNS.values())[:k]) for k in range(len(COLUMNS))]
N_COLUMNS = sum(COLUMNS.values())
DVE_F, DVE_B = 79, 52
ACT_F, ACT_B = 2, 1 + STATES


def kernel(**inputs):
    import concourse.bacc as bacc
    from concourse.bass_utils import run_bass_kernel_spmd

    a = {k: np.ascontiguousarray(v) for k, v in inputs.items()}
    a["columns"] = np.ascontiguousarray(np.concatenate([a.pop(k).reshape(-1, P).T for k in COLUMNS], axis=1))
    w2 = np.asarray(a["L0_ffn_w2"])
    a["w1T"] = np.ascontiguousarray(a.pop("L0_ffn_w1").T)
    a["w2T"] = np.ascontiguousarray(w2.T.reshape(HC, P, D).transpose(1, 0, 2).reshape(P, HC * D))
    a.pop("L0_ffn_w2")
    a["moe_b2T"] = np.ascontiguousarray(a.pop("L1_ffn_b2").T)
    a["mamba_W_inT"] = np.ascontiguousarray(a.pop("L1_attn_W_in").T)
    a["mamba_W_xT"] = np.ascontiguousarray(a.pop("L1_attn_W_x").T)
    a["mamba_W_dtT"] = np.ascontiguousarray(a.pop("L1_attn_W_dt").T)
    a["mamba_W_outT"] = np.ascontiguousarray(a.pop("L1_attn_W_out").T)
    nc = bacc.Bacc("TRN2", target_bir_lowering=False, num_devices=1)
    A = {k: nc.dram_tensor(k, v.shape, F32, kind="ExternalInput").ap() for k, v in a.items()}
    out = nc.dram_tensor("out", (BATCH, SEQ, D), F32, kind="ExternalOutput").ap()
    build(nc, A, out)
    r = run_bass_kernel_spmd(nc, [a], core_ids=[0])
    return r.results[0]["out"]
```
